# Optimizing a Trainium2 kernel written in Bass

```python
import numpy as np
import jax
import jax.numpy as jnp

def _softmax(x, axis=-1):
    return jax.nn.softmax(x, axis=axis)

def _gelu(x):
    return jax.nn.gelu(x, approximate=True)

def _silu(x):
    return jax.nn.silu(x)

def _sigmoid(x):
    return jax.nn.sigmoid(x)

def _layernorm(x, axis=-1, eps=1e-05):
    m = jnp.mean(x, axis=axis, keepdims=True)
    v = jnp.var(x, axis=axis, keepdims=True)
    return (x - m) / jnp.sqrt(v + eps)

def _scatter_add(tgt, idx, src, axis=0):
    return tgt.at[idx].add(src)

def _segment_sum(src, seg, n):
    return jax.ops.segment_sum(src, seg, n)
kernel_name = 'mk_gnn_preln_d2_gnn_r64_6399ad'

def setup_inputs(seed: int=0):
    np.random.seed(seed)
    _w = jnp.asarray

    def _rec_inputs():
        import jax
        import jax.numpy as jnp
        _gk = jax.random.key(seed)
        x = -0.0008691 + 1 * jax.random.normal(jax.random.fold_in(_gk, 1), (100000, 128), jnp.float32)
        _s = jax.random.randint(jax.random.fold_in(_gk, 2), (12500,), 0, 100000, jnp.int32)
        _d = jax.random.randint(jax.random.fold_in(_gk, 3), (12500,), 0, 100000, jnp.int32)
        _loop = jnp.arange(100000, dtype=jnp.int32)
        src = jnp.concatenate([_s, _d, _loop])
        dst = jnp.concatenate([_d, _s, _loop])
        _o = jnp.argsort(dst, stable=True)
        src = src[_o]
        dst = dst[_o]
        return (x, src, dst)
    x, src, dst = _rec_inputs()

    def _L0_gnn_setup():
        import jax, jax.numpy as jnp
        import numpy as np
        N = 10000
        E = 10000
        D_IN = 128
        D_OUT = 128
        key = jax.random.key(seed)
        k1, k2, k3, k4, k5, k6 = jax.random.split(key, 6)
        x = jax.random.normal(k1, (N, D_IN), dtype=jnp.float32)
        edge_index = jax.random.randint(k2, (2, E), 0, N, dtype=jnp.int64)
        s = 1.0 / np.sqrt(D_IN)
        W_self = jax.random.uniform(k3, (D_OUT, D_IN), jnp.float32, -s, s)
        b_self = jax.random.uniform(k4, (D_OUT,), jnp.float32, -s, s)
        W_neigh = jax.random.uniform(k5, (D_OUT, D_IN), jnp.float32, -s, s)
        b_neigh = jax.random.uniform(k6, (D_OUT,), jnp.float32, -s, s)
        return {'x': x, 'edge_index': edge_index, 'W_self': W_self, 'b_self': b_self, 'W_neigh': W_neigh, 'b_neigh': b_neigh}
    _L0_gnn_all = _L0_gnn_setup()
    _L0_gnn_in = {k: v for k, v in _L0_gnn_all.items() if k in ('W_self', 'b_self', 'W_neigh', 'b_neigh')}
    del _L0_gnn_all

    def _L1_gnn_setup():
        import jax, jax.numpy as jnp
        import numpy as np
        N_NODES = 100000
        N_EDGES = 9375
        D_FEAT = 128
        key = jax.random.key(seed)
        k1, k2 = jax.random.split(key)
        x = jax.random.normal(k1, (N_NODES, D_FEAT), dtype=jnp.float32)
        edge_index = jax.random.randint(k2, (2, N_EDGES), 0, N_NODES, dtype=jnp.int64)
        return {'x': x, 'edge_index': edge_index}
    _L1_gnn_all = _L1_gnn_setup()
    _L1_gnn_in = {k: v for k, v in _L1_gnn_all.items() if k in ()}
    del _L1_gnn_all
    return {'x': x, 'src': src, 'dst': dst, 'L0_gnn_W_self': _L0_gnn_in['W_self'], 'L0_gnn_b_self': _L0_gnn_in['b_self'], 'L0_gnn_W_neigh': _L0_gnn_in['W_neigh'], 'L0_gnn_b_neigh': _L0_gnn_in['b_neigh']}

def reference(x, src, dst, L0_gnn_W_self, L0_gnn_b_self, L0_gnn_W_neigh, L0_gnn_b_neigh):
    import jax
    import jax.numpy as jnp

    def _L0_gnn_ref(x, edge_index, W_self, b_self, W_neigh, b_neigh):
        import jax, jax.numpy as jnp
        import numpy as np
        N = 10000
        E = 10000
        D_IN = 128
        D_OUT = 128
        row, col = (edge_index[0], edge_index[1])
        n = x.shape[0]
        out = x @ W_self.T + b_self
        neigh = x[col] @ W_neigh.T + b_neigh
        agg = jax.ops.segment_sum(neigh, row, num_segments=n)
        count = jax.ops.segment_sum(jnp.ones((row.shape[0],), dtype=x.dtype), row, num_segments=n)
        count = jnp.clip(count, 1.0, None)[:, None]
        return out + agg / count

    def _L1_gnn_ref(x, edge_index):
        import jax, jax.numpy as jnp
        import numpy as np
        N_NODES = 100000
        N_EDGES = 9375
        D_FEAT = 128
        src = edge_index[0]
        dst = edge_index[1]
        n = x.shape[0]
        deg = jax.ops.segment_sum(jnp.ones_like(src, dtype=x.dtype), dst, num_segments=n)
        deg_inv_sqrt = jnp.where(deg > 0, jax.lax.rsqrt(jnp.maximum(deg, 1.0)) * jnp.where(deg > 0, 1.0, 0.0) + 0.0, 0.0)
        deg_inv_sqrt = jnp.where(deg > 0, deg ** (-0.5), 0.0)
        norm = deg_inv_sqrt[src] * deg_inv_sqrt[dst]
        msgs = x[src] * norm[:, None]
        out = jax.ops.segment_sum(msgs, dst, num_segments=n)
        return jax.nn.relu(out)
    edge_index = jnp.stack([src, dst])
    h = jnp.maximum(_layernorm(x, axis=-1), 0.0)
    x = x + _L0_gnn_ref(h, edge_index, L0_gnn_W_self, L0_gnn_b_self, L0_gnn_W_neigh, L0_gnn_b_neigh)
    h = jnp.maximum(_layernorm(x, axis=-1), 0.0)
    x = x + _L1_gnn_ref(h, edge_index)
    return x

_drawn_inputs = setup_inputs


def setup_inputs(seed=0):
    import zlib

    import numpy as np

    out = dict(_drawn_inputs(seed))
    spreads = {}
    factors = {}
    for name, (base, spread) in spreads.items():
        noise = np.random.default_rng([zlib.crc32(name.encode()), seed]).standard_normal(out[name].shape)
        drawn = base * np.exp(spread * noise) if base else spread * noise
        out[name] = jnp.asarray(drawn.astype(out[name].dtype))
    for name, factor in factors.items():
        out[name] = (out[name] * factor).astype(out[name].dtype)
    return out
```

```python
from contextlib import ExitStack

import concourse.bass as bass
from concourse import mybir

f32 = mybir.dt.float32
bf16 = mybir.dt.bfloat16
i32 = mybir.dt.int32
ALU = mybir.AluOpType
ACT = mybir.ActivationFunctionType
AX = mybir.AxisListType

P = 128
D = 128
BT = 8
GT = 4
PAIRS = BT // 2
ROWS = BT + PAIRS
XW = 132
SLOTS = 64
RING = 4
EPS = 1e-5
SHIFT = 17


def gnn(nc, x, src, dst, w_self, b_self, w_neigh, b_neigh, out):
    N, E = x.shape[0], src.shape[0]
    assert N < 1 << SHIFT
    NB = -(-N // (BT * P))
    NT = NB * BT
    LAST = N - BT * P
    BACK = (NB - 1) * BT * P - LAST
    ITERS = (NB - 2) // RING
    assert NB - 2 == ITERS * RING
    ER = 125
    EC = E // ER
    assert ER * EC == E
    TP = 112
    TB = NT // TP
    assert TP * TB == NT
    WIN = P + SLOTS
    EPAD = -(-(E + WIN) // WIN) * WIN
    TAIL = EPAD - E

    def block_rows(i):
        return LAST if isinstance(i, int) and i == NB - 1 else i * (BT * P)

    def first(i, n):
        return isinstance(i, int) and i < n

    x1_table = nc.dram_tensor("x1_table", (N, XW), f32, kind="Internal").ap()
    dst_f = nc.dram_tensor("dst_f", (EPAD,), f32, kind="Internal").ap()
    link_f = nc.dram_tensor("link_f", (EPAD,), f32, kind="Internal").ap()

    ctx = ExitStack()
    with ctx:
        def sb(name, shape, dt=f32):
            return ctx.enter_context(nc.sbuf_tensor(name, shape, dt))

        def ps(name, shape):
            return ctx.enter_context(nc.psum_tensor(name, shape, f32))

        def sem(name):
            return ctx.enter_context(nc.semaphore(name))

        ident = sb("ident", [P, P])
        ones = sb("ones", [P, P])
        halves = sb("halves", [P, 2])
        iota_n = sb("iota_n", [P, P])
        eps = sb("eps", [P, 1])
        wraw = sb("wraw", [P, 2, D])
        wsT = sb("wsT", [P, D])
        wnT = sb("wnT", [P, D])
        brow = sb("brow", [1, 2, D])
        bsum = sb("bsum", [1, 2, D])
        bpart = sb("bpart", [1, 3, GT, D], bf16)
        bias3 = sb("bias3", [3, GT * D], bf16)
        ones3 = sb("ones3", [3, P], bf16)
        es = sb("es", [ER, EC], i32)
        ed = sb("ed", [ER, EC], i32)
        en = sb("en", [ER, EC], i32)
        esf = sb("esf", [ER, EC])
        edf = sb("edf", [ER, EC])
        enf = sb("enf", [ER, EC])
        em = sb("em", [ER, EC])
        tail = sb("tail", [1, 2, TAIL])
        diag = sb("diag", [ER, ER])
        start = sb("start", [TP, TB])
        tnum = sb("tnum", [TP, TB])
        firsts = sb("firsts", [TP, ER])
        below = sb("below", [TP, TB, ER])
        rowf = sb("rowf", [TP, TB])
        rowi = sb("rowi", [TP, TB], i32)
        drow = sb("drow", [TP, TB, EC])
        junk = sb("junk", [TP, EC])
        cnt_in = sb("cnt_in", [TP, TB])
        ptr_f = sb("ptr_f", [TP, TB])
        ptr_i = sb("ptr_i", [TP, TB], i32)
        wd = sb("wd", [TP, TB, WIN])
        wl = sb("wl", [TP, TB, WIN])
        wm = sb("wm", [TP, TB, WIN])
        codes = sb("codes", [TP, TB, SLOTS])
        codei = sb("codei", [TP, TB, SLOTS], i32)
        dli = sb("dli", [TP, TB, SLOTS], i32)
        dl2 = sb("dl2", [TP, TB, 2, SLOTS])
        sr2 = sb("sr2", [TP, TB, 2, SLOTS])
        SRC = sb("SRC", [P, NT // 2], i32)
        DL = sb("DL", [P, NT // 2])
        X = sb("X", [P, RING, ROWS, XW])
        IDX = sb("IDX", [P, RING, PAIRS], i32)
        dls = sb("dls", [P, PAIRS])
        ST = sb("ST", [P, RING, ROWS, 6])
        msum = sb("msum", [P, ROWS])
        mdif = sb("mdif", [P, ROWS])
        m2 = sb("m2", [P, ROWS])
        d24 = sb("d24", [P, ROWS])
        mean = sb("mean", [P, RING, ROWS])
        var = sb("var", [P, RING, ROWS])
        sd = sb("sd", [P, RING, ROWS])
        rstd = sb("rstd", [P, ROWS])
        rs2 = sb("rs2", [P, ROWS])
        H = sb("H", [P, 2, ROWS, D])
        SEL = sb("SEL", [P, 2, PAIRS, P])
        hT = sb("hT", [P, 2, GT * P])
        aT = sb("aT", [P, 2, GT * P])
        deg = sb("deg", [P, BT])
        rc = sb("rc", [P, BT])
        sdeg = sb("sdeg", [P, BT])
        Y = sb("Y", [P, RING, BT, XW])
        R = sb("R", [P, 2, BT, D])

        p_hT = ps("p_hT", [P, GT * P])
        p_aT = [ps(f"p_aT{g}", [P, GT * P]) for g in range(2)]
        p_s = [ps(f"p_s{g}", [P, GT * P]) for g in range(2)]
        p_n = [ps(f"p_n{g}", [P, GT * P]) for g in range(2)]
        p_c = ps("p_c", [P, 512])

        s_edges = sem("edges_loaded")
        s_end = sem("list_end_marked")
        s_w = sem("weights_loaded")
        s_const = sem("consts_ready")
        s_dve = sem("dve_order")
        s_scr = sem("edge_scratch_ready")
        s_scr_st = sem("edge_scratch_stored")
        s_pe0 = sem("pe_setup")
        s_dve0 = sem("dve_setup")
        s_rows = sem("row_numbers_ready")
        s_rowg = sem("rows_gathered")
        s_ptr = sem("pointers_ready")
        s_wing = sem("windows_gathered")
        s_bpart = sem("bias_parts_ready")
        s_bias = sem("bias_placed")
        s_tab = sem("tables_ready")
        x_loaded = [[sem(f"x_loaded{l}_{s}") for s in range(RING)] for l in range(2)]
        gathered = [[sem(f"gathered{l}_{s}") for s in range(RING)] for l in range(2)]
        stored = [[sem(f"stored{l}_{s}") for s in range(RING)] for l in range(2)]
        idx_staged = [sem(f"idx_staged{l}") for l in range(2)]
        idx_seen = [sem(f"idx_seen{l}") for l in range(2)]
        var_ready = [sem(f"var_ready{l}") for l in range(2)]
        sd_ready = [sem(f"sd_ready{l}") for l in range(2)]
        z_ready = [sem(f"z_ready{l}") for l in range(2)]
        h_ready = [sem(f"h_ready{l}") for l in range(2)]
        y_ready = [sem(f"y_ready{l}") for l in range(2)]
        hT_ps = sem("hT_in_psum")
        aT_ps = sem("aT_in_psum")
        hT_sb = sem("hT_in_sbuf")
        aT_sb = sem("aT_in_sbuf")
        deg_ready = sem("deg_ready")
        sdeg_ready = sem("sqrt_deg_ready")
        prod_ready = sem("products_ready")
        prod_used = sem("products_used")
        agg_ready = sem("aggregate_ready")
        r_ready = sem("r_ready")

        block = ctx.enter_context(nc.Block())

        @block.sync
        def _(sp):
            sp.dma_start(es[:, :], src.rearrange("(r c) -> r c", c=EC)).then_inc(s_edges, 16)
            sp.dma_start(ed[:, :], dst.rearrange("(r c) -> r c", c=EC)).then_inc(s_edges, 16)
            sp.wait_ge(s_end, 1)
            sp.dma_start(en[0:ER - 1, :], dst[1:E - EC + 1].rearrange("(r c) -> r c", c=EC)).then_inc(s_edges, 16)
            sp.dma_start(en[ER - 1:ER, 0:EC - 1], dst[E - EC + 1:E].rearrange("(r c) -> r c", r=1)).then_inc(s_edges, 16)
            sp.dma_start(wraw[:, 0, :], w_self).then_inc(s_w, 16)
            sp.dma_start(wraw[:, 1, :], w_neigh).then_inc(s_w, 16)
            sp.dma_start(brow[0:1, 0, :], b_self.rearrange("(a n) -> a n", a=1)).then_inc(s_w, 16)
            sp.dma_start(brow[0:1, 1, :], b_neigh.rearrange("(a n) -> a n", a=1)).then_inc(s_w, 16)

            def load(l, i, s):
                source, w = ((x, D), (x1_table, XW))[l]
                r0 = block_rows(i)
                sp.dma_start(X[:, s, 0:BT, 0:w],
                             source[bass.ds(r0, BT * P), :].rearrange("(j p) d -> p j d", p=P)
                             ).then_inc(x_loaded[l][s], 16)

            def store(l, i, s):
                target, w = ((x1_table, XW), (out, D))[l]
                r0 = block_rows(i)
                sp.dma_start(target[bass.ds(r0, BT * P), :].rearrange("(j p) d -> p j d", p=P),
                             Y[:, s, :, 0:w]).then_inc(stored[l][s], 16)

            for s in range(RING):
                load(0, s, s)
            sp.wait_ge(s_scr, 1)
            sp.dma_start(dst_f[0:E].rearrange("(r c) -> r c", c=EC), edf[:, :]).then_inc(s_scr_st, 16)
            sp.dma_start(link_f[0:E].rearrange("(r c) -> r c", c=EC), em[:, :]).then_inc(s_scr_st, 16)
            sp.dma_start(dst_f[E:EPAD].rearrange("(a c) -> a c", a=1), tail[:, 0, :]).then_inc(s_scr_st, 16)
            sp.dma_start(link_f[E:EPAD].rearrange("(a c) -> a c", a=1), tail[:, 1, :]).then_inc(s_scr_st, 16)
            sp.wait_ge(s_bpart, 1)
            for k in range(3):
                sp.dma_start(bias3[k:k + 1, :], bpart[0:1, k, :, :].rearrange("p a b -> p (a b)")
                             ).then_inc(s_bias, 16)

            for l in range(2):
                if l == 1:
                    for s in range(RING):
                        load(1, s, s)
                with sp.Fori(0, ITERS - 1) as it:
                    for u in range(RING):
                        i = it * RING + u
                        sp.wait_ge(y_ready[l], i + 1)
                        load(l, i + RING, u)
                        store(l, i, u)
                for i in range(RING * (ITERS - 1), NB):
                    sp.wait_ge(y_ready[l], i + 1)
                    if i + RING < NB:
                        load(l, i + RING, i % RING)
                    if i == NB - 1:
                        sp.wait_ge(stored[l][(i - 1) % RING], 16 * ((i - 1) // RING + 1))
                    store(l, i, i % RING)
                for s in range(RING):
                    sp.wait_ge(stored[l][s], 16 * len(range(s, NB, RING)))

        @block.gpsimd
        def _(pool):
            nc.gpsimd.memset(ident[:, :], 0.0).then_inc(s_const, 1)
            nc.gpsimd.iota(iota_n[:, :], pattern=[[1, P]], base=0, channel_multiplier=0,
                           allow_small_or_imprecise_dtypes=True).then_inc(s_const, 1)
            nc.gpsimd.iota(tnum[:, :], pattern=[[TP, TB]], base=0, channel_multiplier=1,
                           allow_small_or_imprecise_dtypes=True).then_inc(s_const, 1)
            pool.wait_ge(s_const, 3)
            nc.gpsimd.affine_select(out=ident[:, :], in_=ident[:, :], compare_op=ALU.not_equal, fill=1.0,
                                    base=0, pattern=[[-1, P]], channel_multiplier=1).then_inc(s_const, 1)
            pool.wait_ge(s_rows, 1)
            pool.wait_ge(s_scr_st, 64)
            for b in range(TB):
                nc.gpsimd.indirect_dma_start(
                    drow[:, b, :], None, dst_f[0:E].rearrange("(r c) -> r c", c=EC),
                    bass.IndirectOffsetOnAxis(ap=rowi[:, b:b + 1], axis=0)).then_inc(s_rowg, 16)
            pool.wait_ge(s_ptr, 1)
            for b in range(TB):
                for win, arr in ((wd, dst_f), (wl, link_f)):
                    nc.gpsimd.indirect_dma_start(
                        win[:, b, :], None, arr.rearrange("(r c) -> r c", c=WIN),
                        bass.IndirectOffsetOnAxis(ap=ptr_i[:, b:b + 1], axis=1)).then_inc(s_wing, 16)
            pool.wait_ge(s_tab, 1)

            def gather(l, i, s):
                nc.gpsimd.tensor_copy(IDX[:, s, :], SRC[:, bass.ds(i * PAIRS, PAIRS)]).then_inc(idx_staged[l], 1)
                pool.wait_ge(idx_staged[l], i + 1)
                pool.sem_inc(idx_seen[l], 1)
                table, w = ((x, D), (x1_table, XW))[l]
                for k in range(PAIRS):
                    nc.gpsimd.indirect_dma_start(
                        X[:, s, BT + k, 0:w], None, table,
                        bass.IndirectOffsetOnAxis(ap=IDX[:, s, k:k + 1], axis=0)).then_inc(gathered[l][s], 16)

            for l in range(2):
                if l == 1:
                    for s in range(RING):
                        pool.wait_ge(stored[0][s], 16 * len(range(s, NB, RING)))
                for s in range(RING):
                    gather(l, s, s)
                with pool.Fori(0, ITERS - 1) as it:
                    for u in range(RING):
                        i = it * RING + u
                        pool.wait_ge(z_ready[l], i + 1)
                        if l == 1:
                            pool.wait_ge(y_ready[l], i + 1)
                        gather(l, i + RING, u)
                for i in range(RING * (ITERS - 1), NB - RING):
                    pool.wait_ge(z_ready[l], i + 1)
                    gather(l, i + RING, i % RING)

        @block.scalar
        def _(act):
            act.wait_ge(s_pe0, 2)
            nc.scalar.copy(wsT[:, :], p_s[0][:, 0:D])
            nc.scalar.copy(wnT[:, :], p_s[1][:, 0:D]).then_inc(s_dve0, 1)
            act.wait_ge(s_const, 4)

            def root(l, i, s):
                act.wait_ge(var_ready[l], i + 1)
                nc.scalar.activation(sd[:, s, :], var[:, s, :], ACT.Sqrt, bias=eps[:, 0:1]).then_inc(sd_ready[l], 1)

            def relu(l, i, p):
                act.wait_ge(z_ready[l], i + 1)
                for c in range(0, ROWS, 4):
                    v = H[:, p, c:c + 4, :].rearrange("p a b -> p (a b)")
                    last = nc.scalar.activation(v, v, ACT.Relu)
                last.then_inc(h_ready[l], 1)

            def evac0(i, u):
                for g in range(2):
                    act.wait_ge(hT_ps, 2 * i + g + 1)
                    if not first(i, 1):
                        act.wait_ge(prod_ready, 2 * i + g - 1)
                    nc.scalar.copy(hT[:, g, :], p_hT[:, :]).then_inc(hT_sb, 1)
                act.wait_ge(aT_ps, i + 1)
                for g in range(2):
                    nc.scalar.copy(aT[:, g, :], p_aT[g][:, :]).then_inc(aT_sb, 1)
                act.wait_ge(deg_ready, i + 1)
                nc.scalar.activation(sdeg[:, :], deg[:, :], ACT.Sqrt).then_inc(sdeg_ready, 1)

            def evac1(i, u):
                for g in range(2):
                    act.wait_ge(agg_ready, i + 1)
                    if not first(i, 2):
                        act.wait_ge(y_ready[1], i - 1)
                    nc.scalar.activation(R[:, u % 2, g:BT:2, :], p_s[g][:, :].rearrange("p (a b) -> p a b", a=GT),
                                         ACT.Relu).then_inc(r_ready, 1)

            for l, evac in ((0, evac0), (1, evac1)):
                root(l, 0, 0)
                root(l, 1, 1)
                relu(l, 0, 0)

                def steady(i, u):
                    root(l, i + 2, (u + 2) % RING)
                    evac(i, u)
                    relu(l, i + 1, (u + 1) % 2)
                for i in range(RING):
                    steady(i, i)
                with act.Fori(1, ITERS) as it:
                    for u in range(RING):
                        steady(it * RING + u, u)
                evac(NB - 2, (NB - 2) % RING)
                relu(l, NB - 1, (NB - 1) % 2)
                evac(NB - 1, (NB - 1) % RING)

        @block.tensor
        def _(pe):
            pe.wait_ge(s_const, 4)
            pe.wait_ge(s_w, 64)
            nc.tensor.transpose(p_s[0][:, 0:D], wraw[:, 0, :], ident[:, :]).then_inc(s_pe0, 1)
            nc.tensor.transpose(p_s[1][:, 0:D], wraw[:, 1, :], ident[:, :]).then_inc(s_pe0, 1)
            pe.wait_ge(s_dve0, 2)
            nc.tensor.matmul(p_c[0:TP, 0:ER], ones[0:ER, 0:TP], diag[:, :], start=True, stop=True).then_inc(s_pe0, 1)
            pe.wait_ge(s_dve0, 4)
            for b in range(TB):
                if b:
                    pe.wait_ge(s_dve0, 4 + b)
                nc.tensor.transpose(p_s[0][:, 0:TP], dl2[:, b, :, :].rearrange("p a b -> p (a b)"), ident[0:TP, 0:TP])
                nc.tensor.transpose(p_s[1][:, 0:TP], sr2[:, b, :, :].rearrange("p a b -> p (a b)"), ident[0:TP, 0:TP]).then_inc(s_pe0, 1)
            pe.wait_ge(s_tab, 1)
            pe.wait_ge(s_bias, 48)

            def turn(i, p):
                pe.wait_ge(h_ready[0], i + 1)
                for g in range(2):
                    if not (first(i, 1) and g == 0):
                        pe.wait_ge(hT_sb, 2 * i + g)
                    for j in range(GT):
                        last = nc.tensor.transpose(p_hT[:, P * j:P * j + P], H[:, p, 2 * j + g, :], ident[:, :])
                    last.then_inc(hT_ps, 1)
                    if not first(i, 1):
                        pe.wait_ge(aT_sb, 2 * i + g - 1)
                        if g == 0:
                            pe.wait_ge(deg_ready, i)
                    for j in range(GT):
                        nc.tensor.matmul(p_aT[g][:, P * j:P * j + P], H[:, p, 2 * j + g, :], ident[:, :],
                                         start=(j == 0), stop=False, is_transpose=True, skip_group_check=True)
                for j in range(GT):
                    for g in range(2):
                        q = slice(SLOTS * g, SLOTS * g + SLOTS)
                        last = nc.tensor.matmul(p_aT[g][:, P * j:P * j + P], H[q, p, BT + j, :], SEL[q, p, j, :],
                                                start=False, stop=(j == GT - 1), skip_group_check=True)
                for j in range(PAIRS):
                    last = nc.tensor.matmul(p_c[:, 2 * j:2 * j + 2], SEL[:, p, j, :], halves[:, :], start=True, stop=True)
                last.then_inc(aT_ps, 1)

            def products(i):
                for g in range(2):
                    if not first(i, 1):
                        pe.wait_ge(prod_used, 2 * i + g - 1)
                    pe.wait_ge(hT_sb, 2 * i + g + 1)
                    nc.tensor.matmul(p_s[g][:, :], ones3[:, :], bias3[:, :], start=True, stop=False)
                    for j in range(GT):
                        c = slice(P * j, P * j + P)
                        nc.tensor.matmul(p_s[g][:, c], hT[:, g, c], wsT[:, :], start=False, stop=(j == GT - 1))
                    pe.wait_ge(aT_sb, 2 * i + g + 1)
                    for j in range(GT):
                        c = slice(P * j, P * j + P)
                        last = nc.tensor.matmul(p_n[g][:, c], aT[:, g, c], wnT[:, :], start=True, stop=True)
                    last.then_inc(prod_ready, 1)

            def layer0(i, u):
                turn(i, u % 2)
                products(i)

            def layer1(i, u):
                p = u % 2
                pe.wait_ge(h_ready[1], i + 1)
                for g in range(2):
                    if not first(i, 1):
                        pe.wait_ge(r_ready, 2 * i + g - 1)
                    nc.tensor.matmul(p_s[g][:, :], ident[:, :], H[:, p, g:BT:2, :], start=True, stop=False)
                for j in range(GT):
                    for g in range(2):
                        q = slice(SLOTS * g, SLOTS * g + SLOTS)
                        last = nc.tensor.matmul(p_s[g][:, P * j:P * j + P], SEL[q, p, j, :], H[q, p, BT + j, :],
                                                start=False, stop=(j == GT - 1))
                last.then_inc(agg_ready, 1)

            for body in (layer0, layer1):
                for i in range(RING):
                    body(i, i)
                with pe.Fori(1, ITERS) as it:
                    for u in range(RING):
                        body(it * RING + u, u)
                for i in range(NB - 2, NB):
                    body(i, i % RING)

        @block.vector
        def _(dve):
            steps = [0, None]
            V = nc.vector

            def done(ins):
                steps[0] += 1
                ins.then_inc(s_dve, 1)
                dve.wait_ge(s_dve, steps[0] if steps[1] is None else steps[1] + steps[0])

            V.memset(en[:, EC - 1:EC], -1).then_inc(s_end, 1)
            V.memset(eps[:, :], EPS)
            V.memset(ones3[:, :], 1.0)
            V.memset(tail[:, 0, :], float(4 * N))
            V.memset(tail[:, 1, :], -1.0)
            for s in range(RING):
                V.memset(Y[:, s, :, D:XW], 0.0)
            V.memset(ones[:, :], 1.0)
            done(V.memset(halves[:, :], 0.0))
            V.memset(halves[0:SLOTS, 0:1], 1.0)
            V.memset(halves[SLOTS:P, 1:2], 1.0)
            dve.wait_ge(s_edges, 64)
            V.tensor_copy(esf[:, :], es[:, :])
            V.tensor_copy(enf[:, :], en[:, :])
            done(V.tensor_copy(edf[:, :], ed[:, :]))
            dve.wait_ge(s_const, 4)
            V.tensor_scalar(diag[:, :], ident[0:ER, 0:ER], edf[:, 0:1], None, ALU.mult).then_inc(s_dve0, 1)
            done(V.tensor_tensor(em[:, :], edf[:, :], enf[:, :], ALU.not_equal))
            done(V.tensor_tensor(enf[:, :], esf[:, :], edf[:, :], ALU.is_equal))
            done(V.tensor_tensor(em[:, :], em[:, :], enf[:, :], ALU.mult))
            done(V.tensor_scalar(em[:, :], em[:, :], -1.0, 1.0, ALU.mult, ALU.add))
            done(V.scalar_tensor_tensor(em[:, :], esf[:, :], 1.0, em[:, :], ALU.add, ALU.mult))
            V.tensor_scalar(em[:, :], em[:, :], -1.0, None, ALU.add).then_inc(s_scr, 1)
            done(V.tensor_scalar(start[:, :], tnum[:, :], float(NT - BT), float(-BACK), ALU.is_ge, ALU.mult))
            done(V.scalar_tensor_tensor(start[:, :], tnum[:, :], float(P), start[:, :], ALU.mult, ALU.add))
            dve.wait_ge(s_pe0, 3)
            done(V.tensor_copy(firsts[:, :], p_c[0:TP, 0:ER]))
            done(V.tensor_tensor(below[:, :, :], firsts[:, :].rearrange("p (a c) -> p a c", a=1).to_broadcast([TP, TB, ER]),
                                 start[:, :].rearrange("p (b a) -> p b a", a=1).to_broadcast([TP, TB, ER]), ALU.is_lt))
            done(V.tensor_reduce(rowf[:, :], below[:, :, :], AX.X, ALU.add))
            done(V.tensor_scalar(rowf[:, :], rowf[:, :], -1.0, 0.0, ALU.add, ALU.max))
            V.tensor_copy(rowi[:, :], rowf[:, :]).then_inc(s_rows, 1)
            dve.wait_ge(s_w, 64)
            done(V.tensor_tensor(bsum[0:1, 0, :], brow[0:1, 0, :], brow[0:1, 1, :], ALU.add))
            for k in range(3):
                a, b = bsum[0:1, k % 2, :], bsum[0:1, (k + 1) % 2, :]
                for j in range(GT):
                    last = V.tensor_copy(bpart[0:1, k, j, :], a)
                done(last)
                if k < 2:
                    done(V.tensor_tensor(b, a, bpart[0:1, k, 0, :], ALU.subtract))
            dve.sem_inc(s_bpart, 1)
            dve.wait_ge(s_rowg, 16 * TB)
            for b in range(TB):
                last = V.tensor_scalar(junk[:, :], drow[:, b, :], start[:, b:b + 1], None, ALU.is_lt, ALU.add,
                                       accum_out=cnt_in[:, b:b + 1])
                done(last)
            done(V.scalar_tensor_tensor(ptr_f[:, :], rowf[:, :], float(EC), cnt_in[:, :], ALU.mult, ALU.add))
            V.tensor_copy(ptr_i[:, :], ptr_f[:, :]).then_inc(s_ptr, 1)
            dve.wait_ge(s_wing, 32 * TB)
            done(V.tensor_tensor(wd[:, :, :], wd[:, :, :],
                                 start[:, :].rearrange("p (b a) -> p b a", a=1).to_broadcast([TP, TB, WIN]), ALU.subtract))
            done(V.tensor_scalar(wm[:, :, :], wd[:, :, :], 0.0, None, ALU.is_ge))
            done(V.scalar_tensor_tensor(wm[:, :, :], wd[:, :, :], float(P), wm[:, :, :], ALU.is_lt, ALU.mult))
            done(V.scalar_tensor_tensor(wm[:, :, :], wl[:, :, :], 0.0, wm[:, :, :], ALU.is_ge, ALU.mult))
            done(V.scalar_tensor_tensor(wd[:, :, :], wd[:, :, :], float(1 << SHIFT), wl[:, :, :], ALU.mult, ALU.add))
            done(V.scalar_tensor_tensor(wd[:, :, :], wd[:, :, :], 1.0, wm[:, :, :], ALU.add, ALU.mult))
            done(V.tensor_scalar(wd[:, :, :], wd[:, :, :], -1.0, None, ALU.add))
            for r in range(0, SLOTS, 8):
                for b in range(TB):
                    last = V.max(codes[:, b, r:r + 8], wd[:, b, :])
                done(last)
                for b in range(TB):
                    last = V.match_replace(wd[:, b, :], codes[:, b, r:r + 8], wd[:, b, :], -1.0)
                done(last)
            done(V.tensor_copy(codei[:, :, :], codes[:, :, :]))
            V.tensor_scalar(dli[:, :, :], codei[:, :, :], SHIFT, None, ALU.arith_shift_right)
            done(V.tensor_scalar(codei[:, :, :], codei[:, :, :], (1 << SHIFT) - 1, None, ALU.bitwise_and))
            for a in range(2):
                V.tensor_copy(dl2[:, :, a, :], dli[:, :, :])
                last = V.tensor_copy(sr2[:, :, a, :], codei[:, :, :])
            done(last)
            mask = codes
            done(V.tensor_scalar(mask[:, :, :], codes[:, :, :], 0.0, None, ALU.is_ge))
            for a in range(2):
                last = V.tensor_tensor(sr2[:, :, a, :], sr2[:, :, a, :],
                                       start[:, :].rearrange("p (b a) -> p b a", a=1).to_broadcast([TP, TB, SLOTS]), ALU.subtract)
            done(last)
            for a in range(2):
                last = V.tensor_tensor(sr2[:, :, a, :], sr2[:, :, a, :], mask[:, :, :], ALU.mult)
            done(last)
            for a in range(2):
                last = V.tensor_tensor(sr2[:, :, a, :], sr2[:, :, a, :],
                                       start[:, :].rearrange("p (b a) -> p b a", a=1).to_broadcast([TP, TB, SLOTS]), ALU.add)
            last.then_inc(s_dve0, 2)
            HP = TP // 2
            for b in range(TB):
                dve.wait_ge(s_pe0, 4 + b)
                for a in range(2):
                    q = slice(SLOTS * a, SLOTS * a + SLOTS)
                    V.tensor_copy(DL[q, HP * b:HP * b + HP], p_s[0][q, a:TP:2])
                    last = V.tensor_copy(SRC[q, HP * b:HP * b + HP], p_s[1][q, a:TP:2])
                last.then_inc(s_dve0, 1)
            dve.wait_ge(s_dve0, 4 + TB)
            dve.sem_inc(s_tab, 1)

            def place(turn, off):
                return turn * RING + off, off % RING, turn + off // RING + 1

            def stats(l, turn, off):
                i, s, uses = place(turn, off)
                dve.wait_ge(x_loaded[l][s], uses * 16)
                dve.wait_ge(gathered[l][s], uses * (16 * PAIRS))
                for r in range(ROWS):
                    last = V.bn_stats(ST[:, s, r, :], X[:, s, r, 0:D])
                done(last)
                me, m2e, mo, m2o = (ST[:, s, :, k] for k in (1, 2, 4, 5))
                V.tensor_tensor(msum[:, :], me, mo, ALU.add)
                V.tensor_tensor(mdif[:, :], me, mo, ALU.subtract)
                done(V.tensor_tensor(m2[:, :], m2e, m2o, ALU.add))
                V.tensor_scalar(mean[:, s, :], msum[:, :], 0.5, None, ALU.mult)
                done(V.scalar_tensor_tensor(d24[:, :], mdif[:, :], 0.25, mdif[:, :], ALU.mult, ALU.mult))
                V.scalar_tensor_tensor(var[:, s, :], m2[:, :], 1.0 / D, d24[:, :], ALU.mult, ALU.add
                                       ).then_inc(var_ready[l], 1)

            def free(l, i):
                if first(i, 2):
                    return
                if l == 0:
                    dve.wait_ge(aT_ps, i - 1)
                else:
                    dve.wait_ge(agg_ready, i - 1)

            def normalise(l, turn, off):
                i, s, _ = place(turn, off)
                p = s % 2
                free(l, i)
                done(V.tensor_copy(dls[:, :], DL[:, bass.ds(i * PAIRS, PAIRS)]))
                for k in range(PAIRS):
                    V.tensor_scalar(SEL[:, p, k, :], iota_n[:, :], dls[:, k:k + 1], None, ALU.is_equal)
                dve.wait_ge(sd_ready[l], i + 1)
                done(V.reciprocal(rstd[:, :], sd[:, s, :]))
                scale = rstd
                if l == 1:
                    done(V.tensor_tensor(rs2[:, :], rstd[:, :], X[:, s, :, D], ALU.mult))
                    scale = rs2
                for r in range(ROWS):
                    last = V.tensor_scalar(H[:, p, r, :], X[:, s, r, 0:D], mean[:, s, r:r + 1], scale[:, r:r + 1],
                                           ALU.subtract, ALU.mult)
                last.then_inc(z_ready[l], 1)

            def finish0(turn, off):
                i, s, uses = place(turn, off)
                if not first(i, RING):
                    dve.wait_ge(stored[0][s], uses * 16 - 16)
                dve.wait_ge(aT_ps, i + 1)
                if not first(i, 1):
                    dve.wait_ge(sdeg_ready, i)
                done(V.tensor_scalar(deg[:, :], p_c[:, 0:BT], 1.0, None, ALU.add))
                V.reciprocal(rc[:, :], deg[:, :]).then_inc(deg_ready, 1)
                dve.wait_ge(deg_ready, i + 1)
                for g in range(2):
                    dve.wait_ge(prod_ready, 2 * i + g + 1)
                    for j in range(GT):
                        t = 2 * j + g
                        last = V.scalar_tensor_tensor(Y[:, s, t, 0:D], p_n[g][:, P * j:P * j + P], rc[:, t:t + 1],
                                                      X[:, s, t, 0:D], ALU.mult, ALU.add)
                    done(last)
                    o = Y[:, s, g:BT:2, 0:D]
                    V.tensor_tensor(o, o, p_s[g][:, :].rearrange("p (a b) -> p a b", a=GT), ALU.add).then_inc(prod_used, 1)
                dve.wait_ge(sdeg_ready, i + 1)
                V.reciprocal(Y[:, s, :, D], sdeg[:, :]).then_inc(y_ready[0], 1)

            def finish1(turn, off):
                i, s, uses = place(turn, off)
                if first(i, RING):
                    dve.wait_ge(stored[0][s], 16 * len(range(s, NB, RING)))
                else:
                    dve.wait_ge(stored[1][s], uses * 16 - 16)
                for g in range(2):
                    dve.wait_ge(r_ready, 2 * i + g + 1)
                    for j in range(GT):
                        t = 2 * j + g
                        last = V.scalar_tensor_tensor(Y[:, s, t, 0:D], R[:, s % 2, t, :], X[:, s, t, D:D + 1],
                                                      X[:, s, t, 0:D], ALU.mult, ALU.add)
                last.then_inc(y_ready[1], 1)

            for l, finish in ((0, finish0), (1, finish1)):
                def steady(turn, off):
                    stats(l, turn, off + 2)
                    normalise(l, turn, off + 1)
                    finish(turn, off)

                stats(l, 0, 0)
                stats(l, 0, 1)
                normalise(l, 0, 0)
                before = steps[0]
                for u in range(RING):
                    steady(0, u)
                per_turn = steps[0] - before
                at = steps[0]
                with dve.Fori(1, ITERS) as it:
                    steps[1] = (it - 1) * per_turn
                    for u in range(RING):
                        steady(it, u)
                steps[1] = None
                assert steps[0] == at + per_turn
                steps[0] += (ITERS - 2) * per_turn
                normalise(l, 0, NB - 1)
                finish(0, NB - 2)
                finish(0, NB - 1)


_INS = ['x', 'src', 'dst', 'L0_gnn_W_self', 'L0_gnn_b_self', 'L0_gnn_W_neigh', 'L0_gnn_b_neigh']


def kernel(**inputs):
    import numpy as _np
    import concourse.bacc as _bacc
    from concourse.bass_utils import run_bass_kernel_spmd as _run

    nc = _bacc.Bacc("TRN2", target_bir_lowering=False, num_devices=1)
    arrays, args = {}, []
    for name in _INS:
        a = _np.ascontiguousarray(inputs[name])
        arrays[f"in_{name}"] = a
        args.append(nc.dram_tensor(f"in_{name}", a.shape, mybir.dt.from_np(a.dtype), kind="ExternalInput").ap())
    out = nc.dram_tensor("out_x", arrays["in_x"].shape, f32, kind="ExternalOutput").ap()
    gnn(nc, *args, out)
    r = _run(nc, [arrays], core_ids=[0])
    return r.results[0]["out_x"]
```

```python
from contextlib import ExitStack

import concourse.bass as bass
from concourse import mybir

f32 = mybir.dt.float32
bf16 = mybir.dt.bfloat16
i32 = mybir.dt.int32
ALU = mybir.AluOpType
ACT = mybir.ActivationFunctionType
AX = mybir.AxisListType

P = 128
D = 128
BT = 8
GT = 4
PAIRS = BT // 2
ROWS = BT + PAIRS
XW = 132
SLOTS = 64
RING = 6
HR = 3
AHEAD = 5
EPS = 1e-5
SHIFT = 17


def gnn(nc, x, src, dst, w_self, b_self, w_neigh, b_neigh, out):
    N, E = x.shape[0], src.shape[0]
    assert N < 1 << SHIFT
    NB = -(-N // (BT * P))
    NT = NB * BT
    LAST = N - BT * P
    BACK = (NB - 1) * BT * P - LAST
    ITERS = (NB - 5) // RING
    ER = 125
    EC = E // ER
    assert ER * EC == E
    TP = 112
    TB = NT // TP
    assert TP * TB == NT
    WIN = P + SLOTS
    EPAD = -(-(E + WIN) // WIN) * WIN
    TAIL = EPAD - E

    def block_rows(i):
        return LAST if isinstance(i, int) and i == NB - 1 else i * (BT * P)

    def first(i, n):
        return isinstance(i, int) and i < n

    def place(turn, off):
        return turn * RING + off, off % RING, turn + off // RING + 1

    def there(turn, off):
        return not isinstance(turn, int) or 0 <= turn * RING + off < NB

    def schedule(eng, step):
        for off in range(-AHEAD, RING):
            step(0, off)
        with eng.Fori(1, ITERS) as turn:
            for off in range(RING):
                step(turn, off)
        for off in range(ITERS * RING, NB + 1):
            step(0, off)

    x1_table = nc.dram_tensor("x1_table", (N, XW), f32, kind="Internal").ap()
    dst_f = nc.dram_tensor("dst_f", (EPAD,), f32, kind="Internal").ap()
    link_f = nc.dram_tensor("link_f", (EPAD,), f32, kind="Internal").ap()

    ctx = ExitStack()
    with ctx:
        def sb(name, shape, dt=f32):
            return ctx.enter_context(nc.sbuf_tensor(name, shape, dt))

        def ps(name, shape):
            return ctx.enter_context(nc.psum_tensor(name, shape, f32))

        def sem(name):
            return ctx.enter_context(nc.semaphore(name))

        ident = sb("ident", [P, P])
        ones = sb("ones", [P, P])
        quarter = sb("quarter", [P, ROWS])
        halves = sb("halves", [P, 2])
        iota_n = sb("iota_n", [P, P])
        eps = sb("eps", [P, 1])
        wraw = sb("wraw", [P, 2, D])
        wsT = sb("wsT", [P, D])
        wnT = sb("wnT", [P, D])
        brow = sb("brow", [1, 2, D])
        bsum = sb("bsum", [1, 2, D])
        bpart = sb("bpart", [1, 3, GT, D], bf16)
        bias3 = sb("bias3", [3, GT * D], bf16)
        ones3 = sb("ones3", [3, P], bf16)
        es = sb("es", [ER, EC], i32)
        ed = sb("ed", [ER, EC], i32)
        en = sb("en", [ER, EC], i32)
        esf = sb("esf", [ER, EC])
        edf = sb("edf", [ER, EC])
        enf = sb("enf", [ER, EC])
        em = sb("em", [ER, EC])
        tail = sb("tail", [1, 2, TAIL])
        diag = sb("diag", [ER, ER])
        start = sb("start", [TP, TB])
        tnum = sb("tnum", [TP, TB])
        firsts = sb("firsts", [TP, ER])
        below = sb("below", [TP, TB, ER])
        rowf = sb("rowf", [TP, TB])
        rowi = sb("rowi", [TP, TB], i32)
        work = sb("work", [P, TB * EC])
        drow = work[0:TP, :].rearrange("p (b c) -> p b c", b=TB)
        junk = sb("junk", [TP, EC])
        cnt_in = sb("cnt_in", [TP, TB])
        ptr_f = sb("ptr_f", [TP, TB])
        ptr_i = sb("ptr_i", [TP, TB], i32)
        wd = sb("wd", [TP, TB, WIN])
        wl = sb("wl", [TP, TB, WIN])
        wm = sb("wm", [TP, TB, WIN])
        codes = sb("codes", [TP, TB, SLOTS])
        codei = sb("codei", [TP, TB, SLOTS], i32)
        dli = sb("dli", [TP, TB, SLOTS], i32)
        dl2 = sb("dl2", [TP, TB, 2, SLOTS])
        sr2 = sb("sr2", [TP, TB, 2, SLOTS])
        SRC = sb("SRC", [P, NT // 2], i32)
        DL = sb("DL", [P, NT // 2])
        X = sb("X", [P, RING, ROWS, XW])
        IDX = sb("IDX", [P, RING, PAIRS], i32)
        ST = sb("ST", [P, RING, ROWS, 6])
        mdif = sb("mdif", [P, RING, ROWS])
        m2 = sb("m2", [P, RING, ROWS])
        d32 = sb("d32", [P, RING, ROWS])
        msum = sb("msum", [P, RING, ROWS])
        var = sb("var", [P, RING, ROWS])
        sd = sb("sd", [P, RING, ROWS])
        rstd = sb("rstd", [P, RING, ROWS])
        scale = sb("scale", [P, RING, ROWS])
        shift = sb("shift", [P, RING, ROWS])
        HW = HR * ROWS * D
        H = work[:, 0:HW].rearrange("p (a b c) -> p a b c", a=HR, b=ROWS)
        SEL = work[:, HW:HW + HR * PAIRS * P].rearrange("p (a b c) -> p a b c", a=HR, b=PAIRS)
        hT = sb("hT", [P, 2, 2, GT * P])
        aT = sb("aT", [P, 2, 2, GT * P])
        deg = sb("deg", [P, 2, BT])
        rc = sb("rc", [P, 2, BT])
        sdeg = sb("sdeg", [P, 2, BT])
        Y = sb("Y", [P, HR, BT, XW])
        R = sb("R", [P, 2, BT, D])

        p_hT = ps("p_hT", [P, GT * P])
        p_aT = [ps(f"p_aT{g}", [P, GT * P]) for g in range(2)]
        p_s = [ps(f"p_s{g}", [P, GT * P]) for g in range(2)]
        p_n = [ps(f"p_n{g}", [P, GT * P]) for g in range(2)]
        p_c = ps("p_c", [P, 512])

        s_edges = sem("edges_loaded")
        s_end = sem("list_end_marked")
        s_w = sem("weights_loaded")
        s_const = sem("consts_ready")
        s_dve = sem("dve_order")
        s_scr = sem("edge_scratch_ready")
        s_scr_st = sem("edge_scratch_stored")
        s_pe0 = sem("pe_setup")
        s_dve0 = sem("dve_setup")
        s_rows = sem("row_numbers_ready")
        s_rowg = sem("rows_gathered")
        s_ptr = sem("pointers_ready")
        s_wing = sem("windows_gathered")
        s_bpart = sem("bias_parts_ready")
        s_bias = sem("bias_placed")
        s_tab = sem("tables_ready")
        x_loaded = [[sem(f"x_loaded{l}_{s}") for s in range(RING)] for l in range(2)]
        gathered = [[sem(f"gathered{l}_{s}") for s in range(RING)] for l in range(2)]
        stored = [[sem(f"stored{l}_{s}") for s in range(HR)] for l in range(2)]
        idx_staged = [sem(f"idx_staged{l}") for l in range(2)]
        idx_seen = [sem(f"idx_seen{l}") for l in range(2)]
        st_ready = [sem(f"st_ready{l}") for l in range(2)]
        pool_order = [sem(f"pool_order{l}") for l in range(2)]
        var_ready = [sem(f"var_ready{l}") for l in range(2)]
        sd_ready = [sem(f"sd_ready{l}") for l in range(2)]
        norm_ready = [sem(f"norm_ready{l}") for l in range(2)]
        sel_ready = [sem(f"sel_ready{l}") for l in range(2)]
        h_ready = [sem(f"h_ready{l}") for l in range(2)]
        y_ready = [sem(f"y_ready{l}") for l in range(2)]
        hT_ps = sem("hT_in_psum")
        aT_ps = sem("aT_in_psum")
        hT_sb = sem("hT_in_sbuf")
        aT_sb = sem("aT_in_sbuf")
        deg_read = sem("deg_read")
        sdeg_ready = sem("sqrt_deg_ready")
        prod_ready = sem("products_ready")
        prod_used = sem("products_used")
        agg_ready = sem("aggregate_ready")
        r_ready = sem("r_ready")

        block = ctx.enter_context(nc.Block())

        @block.sync
        def _(sp):
            sp.dma_start(es[:, :], src.rearrange("(r c) -> r c", c=EC)).then_inc(s_edges, 16)
            sp.dma_start(ed[:, :], dst.rearrange("(r c) -> r c", c=EC)).then_inc(s_edges, 16)
            sp.wait_ge(s_end, 1)
            sp.dma_start(en[0:ER - 1, :], dst[1:E - EC + 1].rearrange("(r c) -> r c", c=EC)).then_inc(s_edges, 16)
            sp.dma_start(en[ER - 1:ER, 0:EC - 1], dst[E - EC + 1:E].rearrange("(r c) -> r c", r=1)).then_inc(s_edges, 16)
            sp.dma_start(wraw[:, 0, :], w_self).then_inc(s_w, 16)
            sp.dma_start(wraw[:, 1, :], w_neigh).then_inc(s_w, 16)
            sp.dma_start(brow[0:1, 0, :], b_self.rearrange("(a n) -> a n", a=1)).then_inc(s_w, 16)
            sp.dma_start(brow[0:1, 1, :], b_neigh.rearrange("(a n) -> a n", a=1)).then_inc(s_w, 16)

            def load(l, turn, off):
                i, s, _ = place(turn, off)
                source, w = ((x, D), (x1_table, XW))[l]
                r0 = block_rows(i)
                sp.dma_start(X[:, s, 0:BT, 0:w],
                             source[bass.ds(r0, BT * P), :].rearrange("(j p) d -> p j d", p=P)
                             ).then_inc(x_loaded[l][s], 16)

            def store(l, turn, off):
                i, s, _ = place(turn, off)
                target, w = ((x1_table, XW), (out, D))[l]
                r0 = block_rows(i)
                sp.dma_start(target[bass.ds(r0, BT * P), :].rearrange("(j p) d -> p j d", p=P),
                             Y[:, s % HR, :, 0:w]).then_inc(stored[l][s % HR], 16)

            def step(l, turn, off):
                if there(turn, off - 1):
                    sp.wait_ge(y_ready[l], place(turn, off - 1)[0] + 1)
                if there(turn, off + AHEAD) and not (l == 0 and first(turn, 1) and off <= 0):
                    load(l, turn, off + AHEAD)
                if there(turn, off - 1):
                    if first(turn, 1) and off - 1 == NB - 1:
                        sp.wait_ge(stored[l][(NB - 2) % HR], 16 * ((NB - 2) // HR + 1))
                    store(l, turn, off - 1)

            for s in range(RING):
                load(0, 0, s)
            sp.wait_ge(s_scr, 1)
            sp.dma_start(dst_f[0:E].rearrange("(r c) -> r c", c=EC), edf[:, :]).then_inc(s_scr_st, 16)
            sp.dma_start(link_f[0:E].rearrange("(r c) -> r c", c=EC), em[:, :]).then_inc(s_scr_st, 16)
            sp.dma_start(dst_f[E:EPAD].rearrange("(a c) -> a c", a=1), tail[:, 0, :]).then_inc(s_scr_st, 16)
            sp.dma_start(link_f[E:EPAD].rearrange("(a c) -> a c", a=1), tail[:, 1, :]).then_inc(s_scr_st, 16)
            sp.wait_ge(s_bpart, 1)
            for k in range(3):
                sp.dma_start(bias3[k:k + 1, :], bpart[0:1, k, :, :].rearrange("p a b -> p (a b)")
                             ).then_inc(s_bias, 16)

            for l in range(2):
                schedule(sp, lambda turn, off: step(l, turn, off))
                for s in range(HR):
                    sp.wait_ge(stored[l][s], 16 * len(range(s, NB, HR)))

        @block.gpsimd
        def _(pool):
            nc.gpsimd.memset(ident[:, :], 0.0).then_inc(s_const, 1)
            nc.gpsimd.iota(iota_n[:, :], pattern=[[1, P]], base=0, channel_multiplier=0,
                           allow_small_or_imprecise_dtypes=True).then_inc(s_const, 1)
            nc.gpsimd.iota(tnum[:, :], pattern=[[TP, TB]], base=0, channel_multiplier=1,
                           allow_small_or_imprecise_dtypes=True).then_inc(s_const, 1)
            pool.wait_ge(s_const, 3)
            nc.gpsimd.affine_select(out=ident[:, :], in_=ident[:, :], compare_op=ALU.not_equal, fill=1.0,
                                    base=0, pattern=[[-1, P]], channel_multiplier=1).then_inc(s_const, 1)
            pool.wait_ge(s_rows, 1)
            pool.wait_ge(s_scr_st, 64)
            for b in range(TB):
                nc.gpsimd.indirect_dma_start(
                    drow[:, b, :], None, dst_f[0:E].rearrange("(r c) -> r c", c=EC),
                    bass.IndirectOffsetOnAxis(ap=rowi[:, b:b + 1], axis=0)).then_inc(s_rowg, 16)
            pool.wait_ge(s_ptr, 1)
            for b in range(TB):
                for win, arr in ((wd, dst_f), (wl, link_f)):
                    nc.gpsimd.indirect_dma_start(
                        win[:, b, :], None, arr.rearrange("(r c) -> r c", c=WIN),
                        bass.IndirectOffsetOnAxis(ap=ptr_i[:, b:b + 1], axis=1)).then_inc(s_wing, 16)
            pool.wait_ge(s_tab, 1)

            def gather(l, turn, off):
                i, s, _ = place(turn, off)
                if not first(i, RING):
                    pool.wait_ge(h_ready[l], i - RING + 1)
                nc.gpsimd.tensor_copy(IDX[:, s, :], SRC[:, bass.ds(i * PAIRS, PAIRS)]).then_inc(idx_staged[l], 1)
                pool.wait_ge(idx_staged[l], i + 1)
                pool.sem_inc(idx_seen[l], 1)
                table, w = ((x, D), (x1_table, XW))[l]
                for k in range(PAIRS):
                    nc.gpsimd.indirect_dma_start(
                        X[:, s, BT + k, 0:w], None, table,
                        bass.IndirectOffsetOnAxis(ap=IDX[:, s, k:k + 1], axis=0)).then_inc(gathered[l][s], 16)

            def combine(l, turn, off):
                i, s, _ = place(turn, off)
                pool.wait_ge(st_ready[l], i + 1)
                me, m2e, mo, m2o = (ST[:, s, :, k] for k in (1, 2, 4, 5))
                G = nc.gpsimd
                G.tensor_tensor(mdif[:, s, :], me, mo, ALU.subtract)
                G.tensor_tensor(msum[:, s, :], me, mo, ALU.add)
                G.tensor_tensor(m2[:, s, :], m2e, m2o, ALU.add).then_inc(pool_order[l], 1)
                pool.wait_ge(pool_order[l], 3 * i + 1)
                G.tensor_tensor(d32[:, s, :], mdif[:, s, :], mdif[:, s, :], ALU.mult).then_inc(pool_order[l], 1)
                pool.wait_ge(pool_order[l], 3 * i + 2)
                G.tensor_tensor(d32[:, s, :], d32[:, s, :], quarter[:, :], ALU.mult).then_inc(pool_order[l], 1)
                pool.wait_ge(pool_order[l], 3 * i + 3)
                G.tensor_tensor(var[:, s, :], m2[:, s, :], d32[:, s, :], ALU.add).then_inc(var_ready[l], 1)

            def step(l, turn, off):
                if there(turn, off + AHEAD):
                    gather(l, turn, off + AHEAD)
                if there(turn, off + 3):
                    combine(l, turn, off + 3)

            for l in range(2):
                if l == 1:
                    for s in range(HR):
                        pool.wait_ge(stored[0][s], 16 * len(range(s, NB, HR)))
                schedule(pool, lambda turn, off: step(l, turn, off))

        @block.scalar
        def _(act):
            act.wait_ge(s_pe0, 2)
            nc.scalar.copy(wsT[:, :], p_s[0][:, 0:D])
            nc.scalar.copy(wnT[:, :], p_s[1][:, 0:D]).then_inc(s_dve0, 1)
            act.wait_ge(s_const, 4)

            def root(l, turn, off):
                i, s, _ = place(turn, off)
                act.wait_ge(var_ready[l], i + 1)
                nc.scalar.activation(sd[:, s, :], var[:, s, :], ACT.Sqrt, bias=eps[:, 0:1], scale=1.0 / D
                                     ).then_inc(sd_ready[l], 1)

            def normalise(l, turn, off, rows):
                i, s, _ = place(turn, off)
                if rows[0] == 0:
                    act.wait_ge(norm_ready[l], i + 1)
                    if not first(i, HR):
                        act.wait_ge((aT_ps, agg_ready)[l], i - HR + 1)
                for r in rows:
                    last = nc.scalar.activation(H[:, s % HR, r, :], X[:, s, r, 0:D], ACT.Relu,
                                                bias=shift[:, s, r:r + 1], scale=scale[:, s, r:r + 1])
                if rows[-1] == ROWS - 1:
                    last.then_inc(h_ready[l], 1)

            def spill_h(i, s, g):
                act.wait_ge(hT_ps, 2 * i + g + 1)
                if not first(i, 2):
                    act.wait_ge(prod_ready, 2 * i + g - 3)
                nc.scalar.copy(hT[:, s % 2, g, :], p_hT[:, :]).then_inc(hT_sb, 1)

            def spill_a(i, s, g):
                act.wait_ge(aT_ps, i + 1)
                nc.scalar.copy(aT[:, s % 2, g, :], p_aT[g][:, :]).then_inc(aT_sb, 1)

            def step0(turn, off):
                i, s, _ = place(turn, off)
                if there(turn, off + 2):
                    root(0, turn, off + 2)
                if there(turn, off - 1):
                    q = (off - 1) % 2
                    act.wait_ge(deg_read, i)
                    nc.scalar.activation(sdeg[:, q, :], deg[:, q, :], ACT.Sqrt).then_inc(sdeg_ready, 1)
                if there(turn, off):
                    spill_h(i, s, 0)
                if there(turn, off + 1):
                    normalise(0, turn, off + 1, range(0, 5))
                if there(turn, off):
                    spill_h(i, s, 1)
                if there(turn, off + 1):
                    normalise(0, turn, off + 1, range(5, 9))
                if there(turn, off):
                    spill_a(i, s, 0)
                    spill_a(i, s, 1)
                if there(turn, off + 1):
                    normalise(0, turn, off + 1, range(9, ROWS))

            def step1(turn, off):
                i, s, _ = place(turn, off)
                if there(turn, off + 2):
                    root(1, turn, off + 2)
                if there(turn, off + 1):
                    normalise(1, turn, off + 1, range(0, ROWS))
                if there(turn, off):
                    act.wait_ge(agg_ready, i + 1)
                    if not first(i, 2):
                        act.wait_ge(y_ready[1], i - 1)
                    for g in range(2):
                        bank = (p_s, p_n)[s % 2][g]
                        last = nc.scalar.activation(R[:, s % 2, g:BT:2, :], bank[:, :].rearrange("p (a b) -> p a b", a=GT),
                                                    ACT.Relu)
                    last.then_inc(r_ready, 1)

            schedule(act, step0)
            schedule(act, step1)

        @block.tensor
        def _(pe):
            pe.wait_ge(s_const, 4)
            pe.wait_ge(s_w, 64)
            nc.tensor.transpose(p_s[0][:, 0:D], wraw[:, 0, :], ident[:, :]).then_inc(s_pe0, 1)
            nc.tensor.transpose(p_s[1][:, 0:D], wraw[:, 1, :], ident[:, :]).then_inc(s_pe0, 1)
            pe.wait_ge(s_dve0, 2)
            nc.tensor.matmul(p_c[0:TP, 0:ER], ones[0:ER, 0:TP], diag[:, :], start=True, stop=True).then_inc(s_pe0, 1)
            pe.wait_ge(s_dve0, 4)
            for b in range(TB):
                if b:
                    pe.wait_ge(s_dve0, 4 + b)
                nc.tensor.transpose(p_s[0][:, 0:TP], dl2[:, b, :, :].rearrange("p a b -> p (a b)"), ident[0:TP, 0:TP])
                nc.tensor.transpose(p_s[1][:, 0:TP], sr2[:, b, :, :].rearrange("p a b -> p (a b)"), ident[0:TP, 0:TP]).then_inc(s_pe0, 1)
            pe.wait_ge(s_tab, 1)
            pe.wait_ge(s_bias, 48)

            def transpose_h(i, p, g):
                if not (first(i, 1) and g == 0):
                    pe.wait_ge(hT_sb, 2 * i + g)
                for j in range(GT):
                    last = nc.tensor.transpose(p_hT[:, P * j:P * j + P], H[:, p, 2 * j + g, :], ident[:, :])
                last.then_inc(hT_ps, 1)

            def aggregate(i, p, s):
                pe.wait_ge(sel_ready[0], i + 1)
                for j in range(GT):
                    for g in range(2):
                        q = slice(SLOTS * g, SLOTS * g + SLOTS)
                        nc.tensor.matmul(p_aT[g][:, P * j:P * j + P], H[q, p, BT + j, :], SEL[q, p, j, :],
                                         start=False, stop=(j == GT - 1), skip_group_check=True)
                if not first(i, 1):
                    pe.wait_ge(deg_read, i)
                for j in range(PAIRS):
                    c = 2 * j
                    last = nc.tensor.matmul(p_c[:, c:c + 2], SEL[:, p, j, :], halves[:, :], start=True, stop=True)
                last.then_inc(aT_ps, 1)

            def products(turn, off, g):
                i, s, _ = place(turn, off)
                if not first(i, 1):
                    pe.wait_ge(prod_used, 2 * i + g - 1)
                pe.wait_ge(hT_sb, 2 * i + g + 1)
                nc.tensor.matmul(p_s[g][:, :], ones3[:, :], bias3[:, :], start=True, stop=False)
                for j in range(GT):
                    c = slice(P * j, P * j + P)
                    nc.tensor.matmul(p_s[g][:, c], hT[:, s % 2, g, c], wsT[:, :], start=False, stop=(j == GT - 1))
                pe.wait_ge(aT_sb, 2 * i + g + 1)
                for j in range(GT):
                    c = slice(P * j, P * j + P)
                    last = nc.tensor.matmul(p_n[g][:, c], aT[:, s % 2, g, c], wnT[:, :], start=True, stop=True)
                last.then_inc(prod_ready, 1)

            def step0(turn, off):
                i, s, _ = place(turn, off)
                p = s % HR
                if there(turn, off):
                    pe.wait_ge(h_ready[0], i + 1)
                    transpose_h(i, p, 0)
                    if not first(i, 1):
                        pe.wait_ge(aT_sb, 2 * i)
                    for g in range(2):
                        for j in range(GT):
                            nc.tensor.matmul(p_aT[g][:, P * j:P * j + P], H[:, p, 2 * j + g, :], ident[:, :],
                                             start=(j == 0), stop=False, is_transpose=True, skip_group_check=True)
                if there(turn, off - 1):
                    products(turn, off - 1, 0)
                if there(turn, off):
                    transpose_h(i, p, 1)
                    aggregate(i, p, s)
                if there(turn, off - 1):
                    products(turn, off - 1, 1)

            def step1(turn, off):
                i, s, _ = place(turn, off)
                p = s % HR
                if not there(turn, off):
                    return
                banks = (p_s, p_n)[s % 2]
                pe.wait_ge(h_ready[1], i + 1)
                pe.wait_ge(sel_ready[1], i + 1)
                if not first(i, 2):
                    pe.wait_ge(r_ready, i - 1)
                for g in range(2):
                    nc.tensor.matmul(banks[g][:, :], ident[:, :], H[:, p, g:BT:2, :], start=True, stop=False)
                for j in range(GT):
                    for g in range(2):
                        q = slice(SLOTS * g, SLOTS * g + SLOTS)
                        last = nc.tensor.matmul(banks[g][:, P * j:P * j + P], SEL[q, p, j, :], H[q, p, BT + j, :],
                                                start=False, stop=(j == GT - 1))
                last.then_inc(agg_ready, 1)

            schedule(pe, step0)
            schedule(pe, step1)

        @block.vector
        def _(dve):
            steps = [0, None]
            V = nc.vector

            def wait_steps():
                dve.wait_ge(s_dve, steps[0] if steps[1] is None else steps[1] + steps[0])

            def done(ins):
                steps[0] += 1
                ins.then_inc(s_dve, 1)
                wait_steps()

            V.memset(en[:, EC - 1:EC], -1).then_inc(s_end, 1)
            V.memset(eps[:, :], EPS)
            V.memset(ones3[:, :], 1.0)
            V.memset(tail[:, 0, :], float(4 * N))
            V.memset(tail[:, 1, :], -1.0)
            for s in range(HR):
                V.memset(Y[:, s, :, D:XW], 0.0)
            V.memset(ones[:, :], 1.0)
            V.memset(quarter[:, :], D / 4.0)
            done(V.memset(halves[:, :], 0.0))
            V.memset(halves[0:SLOTS, 0:1], 1.0)
            V.memset(halves[SLOTS:P, 1:2], 1.0)
            dve.wait_ge(s_edges, 64)
            V.tensor_copy(esf[:, :], es[:, :])
            V.tensor_copy(enf[:, :], en[:, :])
            done(V.tensor_copy(edf[:, :], ed[:, :]))
            dve.wait_ge(s_const, 4)
            V.tensor_scalar(diag[:, :], ident[0:ER, 0:ER], edf[:, 0:1], None, ALU.mult).then_inc(s_dve0, 1)
            done(V.tensor_tensor(em[:, :], edf[:, :], enf[:, :], ALU.not_equal))
            done(V.tensor_tensor(enf[:, :], esf[:, :], edf[:, :], ALU.is_equal))
            done(V.tensor_tensor(em[:, :], em[:, :], enf[:, :], ALU.mult))
            done(V.tensor_scalar(em[:, :], em[:, :], -1.0, 1.0, ALU.mult, ALU.add))
            done(V.scalar_tensor_tensor(em[:, :], esf[:, :], 1.0, em[:, :], ALU.add, ALU.mult))
            V.tensor_scalar(em[:, :], em[:, :], -1.0, None, ALU.add).then_inc(s_scr, 1)
            done(V.tensor_scalar(start[:, :], tnum[:, :], float(NT - BT), float(-BACK), ALU.is_ge, ALU.mult))
            done(V.scalar_tensor_tensor(start[:, :], tnum[:, :], float(P), start[:, :], ALU.mult, ALU.add))
            dve.wait_ge(s_pe0, 3)
            done(V.tensor_copy(firsts[:, :], p_c[0:TP, 0:ER]))
            done(V.tensor_tensor(below[:, :, :], firsts[:, :].rearrange("p (a c) -> p a c", a=1).to_broadcast([TP, TB, ER]),
                                 start[:, :].rearrange("p (b a) -> p b a", a=1).to_broadcast([TP, TB, ER]), ALU.is_lt))
            done(V.tensor_reduce(rowf[:, :], below[:, :, :], AX.X, ALU.add))
            done(V.tensor_scalar(rowf[:, :], rowf[:, :], -1.0, 0.0, ALU.add, ALU.max))
            V.tensor_copy(rowi[:, :], rowf[:, :]).then_inc(s_rows, 1)
            dve.wait_ge(s_w, 64)
            done(V.tensor_tensor(bsum[0:1, 0, :], brow[0:1, 0, :], brow[0:1, 1, :], ALU.add))
            for k in range(3):
                a, b = bsum[0:1, k % 2, :], bsum[0:1, (k + 1) % 2, :]
                for j in range(GT):
                    last = V.tensor_copy(bpart[0:1, k, j, :], a)
                done(last)
                if k < 2:
                    done(V.tensor_tensor(b, a, bpart[0:1, k, 0, :], ALU.subtract))
            dve.sem_inc(s_bpart, 1)
            dve.wait_ge(s_rowg, 16 * TB)
            for b in range(TB):
                last = V.tensor_scalar(junk[:, :], drow[:, b, :], start[:, b:b + 1], None, ALU.is_lt, ALU.add,
                                       accum_out=cnt_in[:, b:b + 1])
                done(last)
            done(V.scalar_tensor_tensor(ptr_f[:, :], rowf[:, :], float(EC), cnt_in[:, :], ALU.mult, ALU.add))
            V.tensor_copy(ptr_i[:, :], ptr_f[:, :]).then_inc(s_ptr, 1)
            dve.wait_ge(s_wing, 32 * TB)
            done(V.tensor_tensor(wd[:, :, :], wd[:, :, :],
                                 start[:, :].rearrange("p (b a) -> p b a", a=1).to_broadcast([TP, TB, WIN]), ALU.subtract))
            done(V.tensor_scalar(wm[:, :, :], wd[:, :, :], 0.0, None, ALU.is_ge))
            done(V.scalar_tensor_tensor(wm[:, :, :], wd[:, :, :], float(P), wm[:, :, :], ALU.is_lt, ALU.mult))
            done(V.scalar_tensor_tensor(wm[:, :, :], wl[:, :, :], 0.0, wm[:, :, :], ALU.is_ge, ALU.mult))
            done(V.scalar_tensor_tensor(wd[:, :, :], wd[:, :, :], float(1 << SHIFT), wl[:, :, :], ALU.mult, ALU.add))
            done(V.scalar_tensor_tensor(wd[:, :, :], wd[:, :, :], 1.0, wm[:, :, :], ALU.add, ALU.mult))
            done(V.tensor_scalar(wd[:, :, :], wd[:, :, :], -1.0, None, ALU.add))
            for r in range(0, SLOTS, 8):
                for b in range(TB):
                    last = V.max(codes[:, b, r:r + 8], wd[:, b, :])
                done(last)
                for b in range(TB):
                    last = V.match_replace(wd[:, b, :], codes[:, b, r:r + 8], wd[:, b, :], -1.0)
                done(last)
            done(V.tensor_copy(codei[:, :, :], codes[:, :, :]))
            V.tensor_scalar(dli[:, :, :], codei[:, :, :], SHIFT, None, ALU.arith_shift_right)
            done(V.tensor_scalar(codei[:, :, :], codei[:, :, :], (1 << SHIFT) - 1, None, ALU.bitwise_and))
            for a in range(2):
                V.tensor_copy(dl2[:, :, a, :], dli[:, :, :])
                last = V.tensor_copy(sr2[:, :, a, :], codei[:, :, :])
            done(last)
            mask = codes
            done(V.tensor_scalar(mask[:, :, :], codes[:, :, :], 0.0, None, ALU.is_ge))
            for a in range(2):
                last = V.tensor_tensor(sr2[:, :, a, :], sr2[:, :, a, :],
                                       start[:, :].rearrange("p (b a) -> p b a", a=1).to_broadcast([TP, TB, SLOTS]), ALU.subtract)
            done(last)
            for a in range(2):
                last = V.tensor_tensor(sr2[:, :, a, :], sr2[:, :, a, :], mask[:, :, :], ALU.mult)
            done(last)
            for a in range(2):
                last = V.tensor_tensor(sr2[:, :, a, :], sr2[:, :, a, :],
                                       start[:, :].rearrange("p (b a) -> p b a", a=1).to_broadcast([TP, TB, SLOTS]), ALU.add)
            last.then_inc(s_dve0, 2)
            HP = TP // 2
            for b in range(TB):
                dve.wait_ge(s_pe0, 4 + b)
                for a in range(2):
                    q = slice(SLOTS * a, SLOTS * a + SLOTS)
                    V.tensor_copy(DL[q, HP * b:HP * b + HP], p_s[0][q, a:TP:2])
                    last = V.tensor_copy(SRC[q, HP * b:HP * b + HP], p_s[1][q, a:TP:2])
                last.then_inc(s_dve0, 1)
            dve.wait_ge(s_dve0, 4 + TB)
            dve.sem_inc(s_tab, 1)

            def stats(l, turn, off):
                i, s, uses = place(turn, off)
                dve.wait_ge(x_loaded[l][s], uses * 16)
                dve.wait_ge(gathered[l][s], uses * (16 * PAIRS))
                for r in range(ROWS):
                    last = V.bn_stats(ST[:, s, r, :], X[:, s, r, 0:D])
                last.then_inc(st_ready[l], 1)

            def inverse(l, turn, off):
                i, s, _ = place(turn, off)
                dve.wait_ge(sd_ready[l], i + 1)
                V.reciprocal((scale, rstd)[l][:, s, :], sd[:, s, :]).then_inc(s_dve, 1)
                steps[0] += 1

            def select(l, turn, off):
                i, s, _ = place(turn, off)
                if not first(i, HR):
                    dve.wait_ge((aT_ps, agg_ready)[l], i - HR + 1)
                V.tensor_tensor(SEL[:, s % HR, :, :],
                                iota_n[:, :].rearrange("p (a n) -> p a n", a=1).to_broadcast([P, PAIRS, P]),
                                DL[:, bass.ds(i * PAIRS, PAIRS)].rearrange("p (a n) -> p a n", n=1).to_broadcast([P, PAIRS, P]),
                                ALU.is_equal).then_inc(sel_ready[l], 1)

            def scales(l, turn, off):
                i, s, _ = place(turn, off)
                wait_steps()
                if l == 1:
                    done(V.tensor_tensor(scale[:, s, :], rstd[:, s, :], X[:, s, :, D], ALU.mult))
                V.scalar_tensor_tensor(shift[:, s, :], msum[:, s, :], -0.5, scale[:, s, :], ALU.mult, ALU.mult
                                       ).then_inc(norm_ready[l], 1)

            def finish0(turn, off):
                i, s, _ = place(turn, off)
                y, p = s % HR, s % 2
                if not first(i, HR):
                    dve.wait_ge(stored[0][y], stores_before(turn, off) * 16)
                for g in range(2):
                    dve.wait_ge(prod_ready, 2 * i + g + 1)
                    for j in range(GT):
                        t = 2 * j + g
                        last = V.scalar_tensor_tensor(Y[:, y, t, 0:D], p_n[g][:, P * j:P * j + P], rc[:, p, t:t + 1],
                                                      X[:, s, t, 0:D], ALU.mult, ALU.add)
                    done(last)
                    o = Y[:, y, g:BT:2, 0:D]
                    last = V.tensor_tensor(o, o, p_s[g][:, :].rearrange("p (a b) -> p a b", a=GT), ALU.add
                                           ).then_inc(prod_used, 1)
                dve.wait_ge(sdeg_ready, i + 1)
                V.reciprocal(Y[:, y, :, D], sdeg[:, p, :]).then_inc(y_ready[0], 1)

            def stores_before(turn, off):
                return turn * (RING // HR) + off // HR

            def counts(turn, off):
                i, s, _ = place(turn, off)
                p = s % 2
                dve.wait_ge(aT_ps, i + 1)
                steps[0] += 1
                if not first(i, 2):
                    dve.wait_ge(sdeg_ready, i - 1)
                V.tensor_scalar(deg[:, p, :], p_c[:, 0:BT], 1.0, None, ALU.add).then_inc(deg_read, 1)
                dve.wait_ge(deg_read, i + 1)
                V.reciprocal(rc[:, p, :], deg[:, p, :]).then_inc(s_dve, 1)
                wait_steps()

            def finish1(turn, off):
                i, s, _ = place(turn, off)
                y = s % HR
                if first(i, HR):
                    dve.wait_ge(stored[0][y], 16 * len(range(y, NB, HR)))
                else:
                    dve.wait_ge(stored[1][y], stores_before(turn, off) * 16)
                dve.wait_ge(r_ready, i + 1)
                for t in range(BT):
                    last = V.scalar_tensor_tensor(Y[:, y, t, 0:D], R[:, s % 2, t, :], X[:, s, t, D:D + 1],
                                                  X[:, s, t, 0:D], ALU.mult, ALU.add)
                last.then_inc(y_ready[1], 1)

            def step(l, turn, off):
                if there(turn, off + 3):
                    stats(l, turn, off + 3)
                if there(turn, off + 2):
                    inverse(l, turn, off + 2)
                if there(turn, off + 1):
                    select(l, turn, off + 1)
                if there(turn, off + 2):
                    scales(l, turn, off + 2)
                if there(turn, off - 1):
                    (finish0, finish1)[l](turn, off - 1)
                if l == 0 and there(turn, off):
                    counts(turn, off)

            PER_STEP = (4, 2)
            for l in range(2):
                for off in range(-AHEAD, RING):
                    step(l, 0, off)
                at = steps[0]
                with dve.Fori(1, ITERS) as turn:
                    steps[1] = (turn - 1) * (RING * PER_STEP[l])
                    for off in range(RING):
                        step(l, turn, off)
                steps[1] = None
                assert steps[0] == at + RING * PER_STEP[l]
                steps[0] += (ITERS - 2) * RING * PER_STEP[l]
                for off in range(ITERS * RING, NB + 1):
                    step(l, 0, off)


_INS = ['x', 'src', 'dst', 'L0_gnn_W_self', 'L0_gnn_b_self', 'L0_gnn_W_neigh', 'L0_gnn_b_neigh']


def kernel(**inputs):
    import numpy as _np
    import concourse.bacc as _bacc
    from concourse.bass_utils import run_bass_kernel_spmd as _run

    nc = _bacc.Bacc("TRN2", target_bir_lowering=False, num_devices=1)
    arrays, args = {}, []
    for name in _INS:
        a = _np.ascontiguousarray(inputs[name])
        arrays[f"in_{name}"] = a
        args.append(nc.dram_tensor(f"in_{name}", a.shape, mybir.dt.from_np(a.dtype), kind="ExternalInput").ap())
    out = nc.dram_tensor("out_x", arrays["in_x"].shape, f32, kind="ExternalOutput").ap()
    gnn(nc, *args, out)
    r = _run(nc, [arrays], core_ids=[0])
    return r.results[0]["out_x"]
```

```python
from contextlib import ExitStack

import concourse.bass as bass
from concourse import mybir

f32 = mybir.dt.float32
bf16 = mybir.dt.bfloat16
i32 = mybir.dt.int32
ALU = mybir.AluOpType
ACT = mybir.ActivationFunctionType
AX = mybir.AxisListType

P = 128
D = 128
BT = 8
GT = 4
PAIRS = BT // 2
ROWS = BT + PAIRS
XW = 132
SLOTS = 64
RING = 6
HR = 3
LAG = (2, 1)
AHEAD = 4
GATHER_AHEAD = (4, 4)
STATS_AHEAD = 3
MID = 7
EPS = 1e-5
SHIFT = 17


def gnn(nc, x, src, dst, w_self, b_self, w_neigh, b_neigh, out):
    N, E = x.shape[0], src.shape[0]
    assert N < 1 << SHIFT
    NB = -(-N // (BT * P))
    NT = NB * BT
    LAST = N - BT * P
    BACK = (NB - 1) * BT * P - LAST
    ITERS = (NB - 5) // RING
    ER = 125
    EC = E // ER
    assert ER * EC == E
    TP = 112
    TB = NT // TP
    assert TP * TB == NT
    WIN = P + SLOTS
    EPAD = -(-(E + WIN) // WIN) * WIN
    TAIL = EPAD - E

    CHECKS = 8
    CUTS = (0, 6, 12)
    HASHES = ((0, 1), (1, 2), (0, 2))
    GROUPS = (range(0, 2), range(2, TB))
    NO_LINK = float(1 << 26)
    TOP = float(P << SHIFT)
    NG = -(-N // P)

    def block_rows(i):
        return LAST if isinstance(i, int) and i == NB - 1 else i * (BT * P)

    def first(i, n):
        return isinstance(i, int) and i < n

    def place(turn, off):
        return turn * RING + off, off % RING, turn + off // RING + 1

    def there(turn, off):
        return not isinstance(turn, int) or 0 <= turn * RING + off < NB

    def schedule(eng, step):
        for off in range(-AHEAD, RING):
            step(0, off)
        with eng.Fori(1, ITERS) as turn:
            for off in range(RING):
                step(turn, off)
        for off in range(ITERS * RING, NB + 2):
            step(0, off)

    def table_parts(table, banks):
        for k, (b0, b1) in enumerate(((0, 4), (4, TB))):
            for a in range(2):
                q = slice(SLOTS * a, SLOTS * a + SLOTS)
                yield (table[q, TP // 2 * b0:TP // 2 * b1].rearrange("p (b t) -> p b t", b=b1 - b0),
                       banks[k][q, 0:TP * (b1 - b0)].rearrange("p (b t a) -> p b t a", b=b1 - b0, a=2)[:, :, :, a])

    def either(eng, fast, general):
        eng.wait_ge(s_flag, 1)
        with eng.If(eng.value_load(flag[0:1, 0:1], min_val=0, max_val=1)):
            fast()
        with eng.Else():
            general()

    x1_table = nc.dram_tensor("x1_table", (N, XW), f32, kind="Internal").ap()
    dst_f = nc.dram_tensor("dst_f", (EPAD,), f32, kind="Internal").ap()
    sum_out = nc.dram_tensor("sum_out", (N, XW), f32, kind="Internal").ap()
    sum_in = nc.dram_tensor("sum_in", (N, XW), f32, kind="Internal").ap()
    link_f = nc.dram_tensor("link_f", (EPAD,), f32, kind="Internal").ap()

    ctx = ExitStack()
    with ctx:
        def sb(name, shape, dt=f32):
            return ctx.enter_context(nc.sbuf_tensor(name, shape, dt))

        def ps(name, shape):
            return ctx.enter_context(nc.psum_tensor(name, shape, f32))

        def sem(name):
            return ctx.enter_context(nc.semaphore(name))

        ident = sb("ident", [P, P])
        ones = sb("ones", [P, P])
        halves = sb("halves", [P, 2], bf16)
        iota_n = sb("iota_n", [P, P])
        eps = sb("eps", [P, 1])
        wraw = sb("wraw", [P, 2, D])
        wsT = sb("wsT", [P, D])
        wnT = sb("wnT", [P, D])
        brow = sb("brow", [1, 2, D])
        bsum = sb("bsum", [1, 2, D])
        bpart = sb("bpart", [1, 3, GT, D], bf16)
        bias3 = sb("bias3", [3, GT * D], bf16)
        ones3 = sb("ones3", [3, P], bf16)
        es = sb("es", [ER, EC], i32)
        ed = sb("ed", [ER, EC], i32)
        en = sb("en", [ER, EC], i32)
        esf = sb("esf", [ER, EC])
        edf = sb("edf", [ER, EC])
        enf = sb("enf", [ER, EC])
        em = sb("em", [ER, EC])
        tail = sb("tail", [1, 2, TAIL])
        diag = sb("diag", [ER, ER])
        start = sb("start", [TP, TB])
        end = sb("end", [TP, TB])
        minus = sb("minus", [TP, TB, SLOTS])
        filler = sb("filler", [TP, TB, SLOTS])
        dis2 = sb("dis2", [TP, TB, 2, SLOTS])
        ones_row = sb("ones_row", [TP, TB * SLOTS])
        tnum = sb("tnum", [TP, TB])
        firsts = sb("firsts", [TP, ER])
        below = sb("below", [TP, TB, ER])
        rowf = sb("rowf", [TP, TB])
        rowi = sb("rowi", [TP, TB], i32)
        work = sb("work", [P, TB * EC])
        drow = work[0:TP, :].rearrange("p (b c) -> p b c", b=TB)
        junk = sb("junk", [TP, EC])
        cnt_in = sb("cnt_in", [TP, TB])
        ptr_f = sb("ptr_f", [TP, TB])
        ptr_i = sb("ptr_i", [TP, TB], i32)
        wd = sb("wd", [TP, TB, WIN])
        wl = sb("wl", [TP, TB, WIN])
        codes = sb("codes", [TP, TB, SLOTS])
        codei = sb("codei", [TP, TB, SLOTS], i32)
        dli = sb("dli", [TP, TB, SLOTS], i32)
        dl2 = sb("dl2", [TP, TB, 2, SLOTS])
        sr2 = sb("sr2", [TP, TB, 2, SLOTS])
        SRC = sb("SRC", [P, NT // 2], i32)
        DL = sb("DL", [P, NT // 2])
        DISL = sb("DISL", [P, NT // 2])
        X = sb("X", [P, RING, ROWS, XW])
        IDX = sb("IDX", [P, RING, PAIRS], i32)
        ST = sb("ST", [P, RING, ROWS, 3])
        sd = sb("sd", [P, RING, ROWS])
        rstd = sb("rstd", [P, RING, ROWS])
        scale = sb("scale", [P, RING, ROWS])
        factor = sb("factor", [P, RING, ROWS])
        shift = sb("shift", [P, RING, ROWS])
        HW = HR * ROWS * D
        H = work[:, 0:HW].rearrange("p (a b c) -> p a b c", a=HR, b=ROWS)
        SEL = work[:, HW:HW + HR * PAIRS * P].rearrange("p (a b c) -> p a b c", a=HR, b=PAIRS)
        SEL_high = work[:, HW:HW + HR * PAIRS * P].bitcast(bf16).rearrange("p (a b c h) -> p a b c h", a=HR, b=PAIRS, h=2)
        sizes = (2 * 2 * GT * P, 2 * 2 * GT * P, HR * BT * XW)
        area = sb("area", [P, max(sum(sizes), 8 * EC)])
        cuts = [sum(sizes[:k]) for k in range(4)]
        hT, aT = (area[:, cuts[k]:cuts[k + 1]].rearrange("p (a b c) -> p a b c", a=2, b=2) for k in range(2))
        Y = area[:, cuts[2]:cuts[3]].rearrange("p (a b c) -> p a b c", a=HR, b=BT)
        digits = area[0:ER, 0:3 * EC].bitcast(bf16).rearrange("p (e k c) -> p e k c", e=2, k=3)
        prod = area[0:ER, 3 * EC:5 * EC].rearrange("p (k c) -> p k c", k=2)
        part = area[0:ER, 6 * EC:8 * EC].bitcast(i32).rearrange("p (k c) -> p k c", k=2)
        diff = sb("diff", [ER, 2, EC])
        checks = sb("checks", [P, CHECKS, 2])
        rowsum = sb("rowsum", [P, CHECKS])
        rowint = sb("rowint", [P, CHECKS, 2], i32)
        verdict = sb("verdict", [1, 4, CHECKS])
        bad = sb("bad", [1, 1])
        flag = sb("flag", [1, 1], i32)
        rc = sb("rc", [P, 2, BT])
        sdeg = sb("sdeg", [P, 2, BT])

        g_at = [0]

        def gen(w, dt=f32):
            v = work[:, g_at[0]:g_at[0] + w]
            g_at[0] += w
            assert g_at[0] <= TB * EC
            return v if dt is f32 else v.bitcast(dt)

        g_rows, g_acc, g_msg, g_new, g_own, g_in, g_y = (gen(XW) for _ in range(7))
        g_diag, g_same, g_h, g_hT, g_aT, g_bs, g_bn, g_t1, g_t2 = (gen(P) for _ in range(9))
        g_zero = gen(BT * XW)
        g_keyf, g_sd, g_rs, g_one = (gen(1) for _ in range(4))
        g_idx = gen(2, i32)
        g_st = gen(6)
        g_mv = gen(2)
        g_c = gen(4)

        p_T = [ps(f"p_T{g}", [P, GT * P]) for g in range(2)]
        p_s = [ps(f"p_s{g}", [P, GT * P]) for g in range(2)]
        p_n = [ps(f"p_n{g}", [P, GT * P]) for g in range(2)]
        p_c = ps("p_c", [P, 512])

        s_edges = sem("edges_loaded")
        s_end = sem("list_end_marked")
        s_dst = sem("dst_float")
        s_next = sem("next_dst_float")
        s_dst_st = sem("dst_stored")
        s_diag = sem("first_dst_on_diagonal")
        s_marks = sem("edges_marked")
        s_part = sem("digit_cut")
        s_full = sem("sums_by_scalar")
        s_src2 = sem("sources_doubled")
        s_dl2 = sem("places_doubled")
        s_w = sem("weights_loaded")
        s_const = sem("consts_ready")
        s_dve = sem("dve_order")
        s_scr = sem("edge_scratch_ready")
        s_scr_st = sem("edge_scratch_stored")
        s_pe0 = sem("pe_setup")
        s_dve0 = sem("dve_setup")
        s_rows = sem("row_numbers_ready")
        s_rowg = [sem(f"rows_gathered{g}") for g in range(2)]
        s_ptr = sem("pointers_ready")
        s_wing = [sem(f"windows_gathered{g}") for g in range(2)]
        s_bsum = sem("bias_rest_ready")
        s_bpart = sem("bias_parts_ready")
        s_bias = sem("bias_placed")
        s_tab = sem("tables_ready")
        s_digits = sem("digits_ready")
        s_prod = sem("check_products_ready")
        s_pool0 = sem("pool_setup")
        s_prod_used = sem("check_products_used")
        s_sums = sem("row_sums_ready")
        s_total = sem("totals_ready")
        s_flag = sem("flag_ready")
        x_loaded = [[sem(f"x_loaded{l}_{s}") for s in range(RING)] for l in range(2)]
        gathered = [[sem(f"gathered{l}_{s}") for s in range(RING)] for l in range(2)]
        stored = [[sem(f"stored{l}_{s}") for s in range(HR)] for l in range(2)]
        idx_staged = [sem(f"idx_staged{l}") for l in range(2)]
        idx_seen = [sem(f"idx_seen{l}") for l in range(2)]
        st_ready = [sem(f"st_ready{l}") for l in range(2)]
        sd_ready = [sem(f"sd_ready{l}") for l in range(2)]
        norm_ready = [sem(f"norm_ready{l}") for l in range(2)]
        row_scaled = [sem(f"last_row_scaled{l}") for l in range(2)]
        row_ready = [sem(f"last_row_ready{l}") for l in range(2)]
        sel_ready = [sem(f"sel_ready{l}") for l in range(2)]
        h_ready = [sem(f"h_ready{l}") for l in range(2)]
        y_ready = [sem(f"y_ready{l}") for l in range(2)]
        hT_ps = sem("hT_in_psum")
        aT_ps = sem("aT_in_psum")
        hT_sb = sem("hT_in_sbuf")
        aT_sb = sem("aT_in_sbuf")
        counts_read = sem("counts_read")
        sdeg_ready = sem("sqrt_deg_ready")
        prod_ready = sem("products_ready")
        prod_used = sem("products_used")
        agg_ready = sem("aggregate_ready")
        s_runs = sem("link_counts_ready")
        s_roots = sem("link_count_roots")
        s_dis2 = sem("link_dis_doubled")
        s_disT = sem("link_dis_in_psum")
        s_disl = sem("link_dis_ready")

        used = dict(idx=(0, 1, 3), got=(0, 2, 3, 4), old=(0, 1, 3), var=(0, 2, 3), sd=(0, 2, 3), msg=(0, 1, 2, 3),
                    diag=(0, 1, 2, 3), keys=(0, 1, 2, 3), same=(0, 1, 3), sum=(0, 1, 3), new=range(5),
                    put=range(5), tT=(2,), tS=(2,), prod=(2,))
        gs = {n: {r: sem(f"g_{n}{r}") for r in rounds} for n, rounds in used.items()}
        g_zeroed = sem("g_zeroed")
        g_clean = sem("g_zero_ready")
        g_ord = sem("g_vector_order")

        block = ctx.enter_context(nc.Block())

        @block.sync
        def _(sp):
            sp.dma_start(es[:, :], src.rearrange("(r c) -> r c", c=EC)).then_inc(s_edges, 16)
            sp.dma_start(ed[:, :], dst.rearrange("(r c) -> r c", c=EC)).then_inc(s_edges, 16)
            sp.wait_ge(s_end, 1)
            sp.dma_start(en[0:ER - 1, :], dst[1:E - EC + 1].rearrange("(r c) -> r c", c=EC)).then_inc(s_edges, 16)
            sp.dma_start(en[ER - 1:ER, 0:EC - 1], dst[E - EC + 1:E].rearrange("(r c) -> r c", r=1)).then_inc(s_edges, 16)
            sp.dma_start(wraw[:, 0, :], w_self).then_inc(s_w, 16)
            sp.dma_start(wraw[:, 1, :], w_neigh).then_inc(s_w, 16)
            sp.dma_start(brow[0:1, 0, :], b_self.rearrange("(a n) -> a n", a=1)).then_inc(s_w, 16)
            sp.dma_start(brow[0:1, 1, :], b_neigh.rearrange("(a n) -> a n", a=1)).then_inc(s_w, 16)

            def load(l, turn, off):
                i, s, _ = place(turn, off)
                source, w = ((x, D), (x1_table, XW))[l]
                r0 = block_rows(i)
                sp.dma_start(X[:, s, 0:BT, 0:w],
                             source[bass.ds(r0, BT * P), :].rearrange("(j p) d -> p j d", p=P)
                             ).then_inc(x_loaded[l][s], 16)

            def store(l, turn, off):
                i, s, _ = place(turn, off)
                target, w = ((x1_table, XW), (out, D))[l]
                r0 = block_rows(i)
                sp.dma_start(target[bass.ds(r0, BT * P), :].rearrange("(j p) d -> p j d", p=P),
                             Y[:, s % HR, :, 0:w]).then_inc(stored[l][s % HR], 16)

            def step(l, turn, off):
                old = off - LAG[l]
                if not there(turn, old):
                    return
                sp.wait_ge(y_ready[l], place(turn, old)[0] + 1)
                if there(turn, old + RING):
                    load(l, turn, old + RING)
                if first(turn, 1) and old == NB - 1:
                    sp.wait_ge(stored[l][(NB - 2) % HR], 16 * ((NB - 2) // HR + 1))
                store(l, turn, old)

            sp.wait_ge(s_dst, 1)
            sp.dma_start(dst_f[0:E].rearrange("(r c) -> r c", c=EC), edf[:, :]).then_inc(s_dst_st, 16)
            sp.dma_start(dst_f[E:EPAD].rearrange("(a c) -> a c", a=1), tail[:, 0, :]).then_inc(s_dst_st, 16)
            sp.wait_ge(s_scr, 1)
            sp.dma_start(link_f[0:E].rearrange("(r c) -> r c", c=EC), esf[:, :]).then_inc(s_scr_st, 16)
            sp.dma_start(link_f[E:EPAD].rearrange("(a c) -> a c", a=1), tail[:, 1, :]).then_inc(s_scr_st, 16)
            sp.wait_ge(s_bpart, 3)
            for k in range(3):
                sp.dma_start(bias3[k:k + 1, :], bpart[0:1, k, :, :].rearrange("p a b -> p (a b)")
                             ).then_inc(s_bias, 16)
            sp.wait_ge(s_ptr, 2)
            for s in range(RING):
                load(0, 0, s)

            def fast():
                for l in range(2):
                    for s in range(RING if l else 0):
                        load(1, 0, s)
                    schedule(sp, lambda turn, off: step(l, turn, off))
                    for s in range(HR):
                        sp.wait_ge(stored[l][s], 16 * len(range(s, NB, HR)))

            def general():
                sp.wait_ge(g_clean, 1)
                for k, table in enumerate((sum_out, sum_in)):
                    with sp.Fori(0, NB - 1) as i:
                        sp.dma_start(table[bass.ds(i * (BT * P), BT * P), :].rearrange("(j p) d -> p j d", p=P),
                                     g_zero.rearrange("p (j d) -> p j d", j=BT)).then_inc(g_zeroed, 16)
                    sp.wait_ge(g_zeroed, 16 * (NB * (k + 1) - 1))
                    sp.dma_start(table[LAST:N, :].rearrange("(j p) d -> p j d", p=P),
                                 g_zero.rearrange("p (j d) -> p j d", j=BT)).then_inc(g_zeroed, 16)
                for r, source, sums, target, w in ((2, x, sum_out, x1_table, XW), (4, x1_table, sum_in, out, D)):
                    sp.wait_ge(gs["put"][r - 1], 16 * EC)

                    def tile(n, r0):
                        v = D if r == 2 else XW
                        if not first(n, 1):
                            sp.wait_ge(gs["put"][r], 16 * n)
                        sp.dma_start(g_rows[:, 0:v], source[bass.ds(r0, P), 0:v]).then_inc(gs["got"][r], 16)
                        sp.dma_start(g_own, sums[bass.ds(r0, P), :]).then_inc(gs["got"][r], 16)
                        sp.dma_start(g_in, sum_in[bass.ds(r0, P), :]).then_inc(gs["got"][r], 16)
                        sp.wait_ge(gs["new"][r], n + 1)
                        sp.dma_start(target[bass.ds(r0, P), :], g_y[:, 0:w]).then_inc(gs["put"][r], 16)

                    tile(0, 0)
                    with sp.Fori(1, NG - 1) as n:
                        tile(n, n * P)
                    tile(NG - 1, N - P)
                    sp.wait_ge(gs["put"][r], 16 * NG)

            either(sp, fast, general)

        @block.gpsimd
        def _(pool):
            nc.gpsimd.memset(ident[:, :], 0.0).then_inc(s_const, 1)
            nc.gpsimd.iota(iota_n[:, :], pattern=[[1, P]], base=0, channel_multiplier=0,
                           allow_small_or_imprecise_dtypes=True).then_inc(s_const, 1)
            nc.gpsimd.iota(tnum[:, :], pattern=[[TP, TB]], base=0, channel_multiplier=1,
                           allow_small_or_imprecise_dtypes=True).then_inc(s_const, 1)
            pool.wait_ge(s_const, 3)
            nc.gpsimd.affine_select(out=ident[:, :], in_=ident[:, :], compare_op=ALU.not_equal, fill=1.0,
                                    base=0, pattern=[[-1, P]], channel_multiplier=1).then_inc(s_const, 1)
            def check_products(k):
                f, g = HASHES[k]
                if k >= 2:
                    pool.wait_ge(s_prod_used, k - 1)
                nc.gpsimd.tensor_tensor(prod[:, 0, :], digits[:, 0, f, :], digits[:, 1, g, :], ALU.mult)
                nc.gpsimd.tensor_tensor(prod[:, 1, :], digits[:, 0, g, :], digits[:, 1, f, :], ALU.mult
                                        ).then_inc(s_pool0, 1)
                pool.wait_ge(s_pool0, 2 * k + 1)
                nc.gpsimd.tensor_tensor(diff[:, k % 2, :], prod[:, 0, :], prod[:, 1, :], ALU.subtract
                                        ).then_inc(s_prod, 1)
                pool.wait_ge(s_prod, k + 1)
                pool.sem_inc(s_pool0, 1)

            pool.wait_ge(s_rows, 1)
            pool.wait_ge(s_dst_st, 32)
            for g, group in enumerate(GROUPS):
                for b in group:
                    nc.gpsimd.indirect_dma_start(
                        drow[:, b, :], None, dst_f[0:E].rearrange("(r c) -> r c", c=EC),
                        bass.IndirectOffsetOnAxis(ap=rowi[:, b:b + 1], axis=0)).then_inc(s_rowg[g], 16)
            pool.wait_ge(s_scr_st, 32)
            for g, group in enumerate(GROUPS):
                pool.wait_ge(s_ptr, g + 1)
                for b in group:
                    for win, arr in ((wd, dst_f), (wl, link_f)):
                        nc.gpsimd.indirect_dma_start(
                            win[:, b, :], None, arr.rearrange("(r c) -> r c", c=WIN),
                            bass.IndirectOffsetOnAxis(ap=ptr_i[:, b:b + 1], axis=1)).then_inc(s_wing[g], 16)
                if g == 0:
                    pool.wait_ge(s_w, 64)
                    nc.gpsimd.tensor_tensor(bsum[0:1, 0, :], brow[0:1, 0, :], brow[0:1, 1, :], ALU.add).then_inc(s_bsum, 1)
                    for k in range(3):
                        a, b = bsum[0:1, k % 2, :], bsum[0:1, (k + 1) % 2, :]
                        pool.wait_ge(s_bsum, k + 1)
                        for j in range(GT):
                            last = nc.gpsimd.tensor_copy(bpart[0:1, k, j, :], a)
                        last.then_inc(s_bpart, 1)
                        if k < 2:
                            pool.wait_ge(s_bpart, k + 1)
                            nc.gpsimd.tensor_tensor(b, a, bpart[0:1, k, 0, :], ALU.subtract).then_inc(s_bsum, 1)
            pool.wait_ge(s_digits, 2 * len(CUTS))
            for k in range(len(HASHES)):
                check_products(k)
            pool.wait_ge(s_tab, 2)

            def stage(l, turn, off):
                i, s, _ = place(turn, off)
                if not first(i, RING):
                    pool.wait_ge(st_ready[l], i - RING + 1)
                    pool.sem_inc(idx_seen[l], 1)
                nc.gpsimd.tensor_copy(IDX[:, s, :], SRC[:, bass.ds(i * PAIRS, PAIRS)]).then_inc(idx_staged[l], 1)

            def may_gather(l, turn, off):
                i, s, _ = place(turn, off)
                if not first(i, RING):
                    pool.wait_ge(h_ready[l], 2 * (i - RING) + 2)
                    pool.sem_inc(idx_seen[l], 1)
                    pool.wait_ge(row_ready[l], i - RING + 1)
                    pool.sem_inc(idx_seen[l], 1)
                pool.wait_ge(idx_staged[l], i + 1)
                pool.sem_inc(idx_seen[l], 1)

            def last_row(turn, off):
                i, s, _ = place(turn, off)
                r = ROWS - 1
                pool.wait_ge(norm_ready[0], i + 1)
                pool.sem_inc(idx_seen[0], 1)
                if not first(i, HR):
                    pool.wait_ge(aT_ps, i - HR + 1)
                    pool.sem_inc(idx_seen[0], 1)
                nc.gpsimd.tensor_scalar(H[:, s % HR, r, :], X[:, s, r, 0:D], scale[:, s, r:r + 1], shift[:, s, r:r + 1],
                                        ALU.mult, ALU.add).then_inc(row_scaled[0], 1)
                pool.wait_ge(row_scaled[0], i + 1)
                pool.sem_inc(idx_seen[0], 1)
                nc.gpsimd.tensor_scalar(H[:, s % HR, r, :], H[:, s % HR, r, :], 0.0, None, ALU.max
                                        ).then_inc(row_ready[0], 1)

            def step(l, turn, off):
                if l == 0 and there(turn, off + 1):
                    last_row(turn, off + 1)
                gathers(l, turn, off + GATHER_AHEAD[l])

            def gathers(l, turn, off):
                i, s, _ = place(turn, off)
                if there(turn, off + 1) and not (first(turn, 1) and off < 0):
                    stage(l, turn, off + 1)
                if not there(turn, off):
                    return
                may_gather(l, turn, off)
                table, w = ((x, D), (x1_table, XW))[l]
                for k in range(PAIRS):
                    nc.gpsimd.indirect_dma_start(
                        X[:, s, BT + k, 0:w], None, table,
                        bass.IndirectOffsetOnAxis(ap=IDX[:, s, k:k + 1], axis=0)).then_inc(gathered[l][s], 16)

            def fast():
                for l in range(2):
                    if l == 1:
                        for s in range(HR):
                            pool.wait_ge(stored[0][s], 16 * len(range(s, NB, HR)))
                    stage(l, 0, 0)
                    schedule(pool, lambda turn, off: step(l, turn, off))

            def general():
                pool.wait_ge(g_zeroed, 16 * 2 * NB)
                for r, table, sums in ((0, x, sum_out), (1, None, sum_in), (3, x1_table, sum_in)):
                    if r == 3:
                        pool.wait_ge(gs["put"][2], 16 * NG)

                    def lot(c):
                        pool.wait_ge(gs["idx"][r], c + 1)
                        pool.sem_inc(idx_seen[0], 1)
                        if table is not None:
                            w = D if r == 0 else XW
                            nc.gpsimd.indirect_dma_start(
                                g_rows[0:ER, 0:w], None, table,
                                bass.IndirectOffsetOnAxis(ap=g_idx[0:ER, 1:2], axis=0)).then_inc(gs["got"][r], 16)
                        if not first(c, 1):
                            pool.wait_ge(gs["put"][r], 16 * c)
                            pool.sem_inc(idx_seen[0], 1)
                        nc.gpsimd.indirect_dma_start(
                            g_acc[0:ER, :], None, sums,
                            bass.IndirectOffsetOnAxis(ap=g_idx[0:ER, 0:1], axis=0)).then_inc(gs["old"][r], 16)
                        pool.wait_ge(gs["new"][r], c + 1)
                        pool.sem_inc(idx_seen[0], 1)
                        nc.gpsimd.indirect_dma_start(
                            sums, bass.IndirectOffsetOnAxis(ap=g_idx[0:ER, 0:1], axis=0),
                            g_new[0:ER, :], None).then_inc(gs["put"][r], 16)

                    lot(0)
                    with pool.Fori(1, EC) as c:
                        lot(c)
                    pool.wait_ge(gs["put"][r], 16 * EC)

            either(pool, fast, general)

        @block.scalar
        def _(act):
            act.wait_ge(s_edges, 64)
            nc.scalar.copy(enf[:, :], en[:, :]).then_inc(s_next, 1)
            act.wait_ge(s_pe0, 2)
            nc.scalar.copy(wsT[:, :], p_s[0][:, 0:D])
            nc.scalar.copy(wnT[:, :], p_s[1][:, 0:D]).then_inc(s_dve0, 1)
            act.wait_ge(s_marks, 1)
            nc.scalar.activation(diff[:, 0, :], diff[:, 0, :], ACT.Copy, accum_out=rowsum[0:ER, 0:1])
            nc.scalar.activation(em[:, :], em[:, :], ACT.Copy, accum_out=rowsum[0:ER, 1:2]).then_inc(s_full, 1)
            for n in range(2 * len(CUTS)):
                act.wait_ge(s_part, n + 1)
                nc.scalar.activation(digits[:, n // 3, n % 3, :], part[:, n % 2, :], ACT.Copy, bias=1.0
                                     ).then_inc(s_digits, 1)
            for k in range(len(HASHES)):
                act.wait_ge(s_prod, k + 1)
                nc.scalar.activation(diff[:, k % 2, :], diff[:, k % 2, :], ACT.Copy, accum_out=rowsum[0:ER, 3 + k:4 + k]
                                     ).then_inc(s_prod_used, 1)
            act.wait_ge(s_dl2, 1)
            nc.scalar.copy(sr2[:, :, :, :], codei[:, :, :].rearrange("p b (a n) -> p b a n", a=1
                                                                     ).to_broadcast([TP, TB, 2, SLOTS])).then_inc(s_src2, 1)
            act.wait_ge(s_pe0, 5)
            for o, i in table_parts(SRC, p_n):
                last = nc.scalar.copy(o, i)
            last.then_inc(s_tab, 1)
            act.wait_ge(s_const, 4)
            act.wait_ge(s_runs, 1)
            nc.scalar.activation(filler[:, :, :], codes[:, :, :], ACT.Sqrt, bias=ones[0:TP, 0:1]).then_inc(s_roots, 1)
            act.wait_ge(s_disT, 1)
            for o, i in table_parts(DISL, p_T):
                last = nc.scalar.copy(o, i)
            last.then_inc(s_disl, 1)

            def root(l, turn, off):
                i, s, _ = place(turn, off)
                act.wait_ge(st_ready[l], i + 1)
                nc.scalar.activation(sd[:, s, :], ST[:, s, :, 2], ACT.Sqrt, bias=eps[:, 0:1], scale=1.0 / D
                                     ).then_inc(sd_ready[l], 1)

            def normalise(l, turn, off, rows):
                i, s, _ = place(turn, off)
                if rows[0] == 0:
                    act.wait_ge(norm_ready[l], i + 1)
                    if not first(i, HR):
                        act.wait_ge((aT_ps, agg_ready)[l], i - HR + 1)
                for r in rows:
                    last = nc.scalar.activation(H[:, s % HR, r, :], X[:, s, r, 0:D], ACT.Relu,
                                                bias=shift[:, s, r:r + 1], scale=scale[:, s, r:r + 1])
                    if r in (BT - 1, ROWS - 2):
                        last.then_inc(h_ready[l], 1)

            def spill_h(i, s, g):
                act.wait_ge(hT_ps, 2 * i + g + 1)
                if not first(i, 2):
                    act.wait_ge(prod_ready, 2 * i + g - 3)
                nc.scalar.copy(hT[:, s % 2, g, :], p_T[g][:, :]).then_inc(hT_sb, 1)

            def spill_a(i, s, g):
                act.wait_ge(aT_ps, i + 1)
                nc.scalar.copy(aT[:, s % 2, g, :], p_T[g][:, :]).then_inc(aT_sb, 1)

            def step0(turn, off):
                i, s, _ = place(turn, off)
                if there(turn, off + 2):
                    root(0, turn, off + 2)
                if there(turn, off):
                    spill_h(i, s, 0)
                    spill_h(i, s, 1)
                if there(turn, off - 1):
                    q = (off - 1) % 2
                    act.wait_ge(counts_read, i)
                    nc.scalar.activation(sdeg[:, q, :], p_c[:, 0:BT], ACT.Sqrt).then_inc(sdeg_ready, 1)
                if there(turn, off + 1):
                    normalise(0, turn, off + 1, range(0, MID))
                if there(turn, off):
                    spill_a(i, s, 0)
                    spill_a(i, s, 1)
                if there(turn, off + 1):
                    normalise(0, turn, off + 1, range(MID, ROWS - 1))

            def step1(turn, off):
                i, s, _ = place(turn, off)
                if there(turn, off + 2):
                    root(1, turn, off + 2)
                if there(turn, off + 1):
                    normalise(1, turn, off + 1, range(0, ROWS - 1))
            def fast():
                schedule(act, step0)
                schedule(act, step1)

            def general():
                for r, n in ((0, EC), (2, NG), (3, EC)):
                    def root_of(c):
                        act.wait_ge(gs["var"][r], c + 1)
                        nc.scalar.activation(g_sd, g_mv[:, 1:2], ACT.Sqrt, bias=eps[:, 0:1]).then_inc(gs["sd"][r], 1)
                        if r == 2:
                            act.wait_ge(gs["diag"][r], c + 1)
                            nc.scalar.activation(g_c[:, 2:3], g_c[:, 1:2], ACT.Sqrt).then_inc(gs["keys"][r], 1)

                    root_of(0)
                    with act.Fori(1, n) as c:
                        root_of(c)

            either(act, fast, general)

        @block.tensor
        def _(pe):
            pe.wait_ge(s_const, 4)
            pe.wait_ge(s_w, 64)
            nc.tensor.transpose(p_s[0][:, 0:D], wraw[:, 0, :], ident[:, :]).then_inc(s_pe0, 1)
            nc.tensor.transpose(p_s[1][:, 0:D], wraw[:, 1, :], ident[:, :]).then_inc(s_pe0, 1)
            pe.wait_ge(s_diag, 1)
            nc.tensor.matmul(p_c[0:TP, 0:ER], ones[0:ER, 0:TP], diag[:, :], start=True, stop=True).then_inc(s_pe0, 1)
            pe.wait_ge(s_dve0, 1)
            for doubled, filled, banks in ((dl2, s_dl2, p_s), (sr2, s_src2, p_n)):
                pe.wait_ge(filled, 2 if filled is s_dl2 else 1)
                for b in range(TB):
                    c = TP * (b % 4)
                    last = nc.tensor.transpose(banks[b // 4][:, c:c + TP],
                                               doubled[:, b, :, :].rearrange("p a b -> p (a b)"), ident[0:TP, 0:TP])
                last.then_inc(s_pe0, 1)
            pe.wait_ge(s_sums, 1)
            nc.tensor.matmul(p_c[0:1, 0:2 * CHECKS], ones[:, 0:1], checks[:, :, :].rearrange("p a b -> p (a b)"),
                             start=True, stop=True).then_inc(s_total, 1)
            pe.wait_ge(s_dis2, 1)
            for b in range(TB):
                c = TP * (b % 4)
                last = nc.tensor.transpose(p_T[b // 4][:, c:c + TP],
                                           dis2[:, b, :, :].rearrange("p a b -> p (a b)"), ident[0:TP, 0:TP])
            last.then_inc(s_disT, 1)
            pe.wait_ge(s_tab, 2)
            pe.wait_ge(s_disl, 1)
            pe.wait_ge(s_bias, 48)

            def transpose_h(i, p, g):
                if not first(i, 1):
                    pe.wait_ge(aT_sb, 2 * i + g - 1)
                for j in range(GT):
                    last = nc.tensor.matmul(p_T[g][:, P * j:P * j + P], H[:, p, 2 * j + g, :], ident[:, :],
                                            start=(j == 0), stop=False, is_transpose=True, skip_group_check=True)
                last.then_inc(hT_ps, 1)

            def aggregate(i, p, s):
                pe.wait_ge(h_ready[0], 2 * i + 2)
                pe.wait_ge(row_ready[0], i + 1)
                pe.wait_ge(sel_ready[0], i + 1)
                pe.wait_ge(hT_sb, 2 * i + 2)
                for j in range(GT):
                    for g in range(2):
                        q = slice(SLOTS * g, SLOTS * g + SLOTS)
                        nc.tensor.matmul(p_T[g][:, P * j:P * j + P], H[q, p, BT + j, :], SEL[q, p, j, :],
                                         start=False, stop=(j == GT - 1), skip_group_check=True)
                if not first(i, 1):
                    pe.wait_ge(sdeg_ready, i)
                for j in range(PAIRS):
                    c = 2 * j
                    nc.tensor.matmul(p_c[:, c:c + 2], SEL_high[:, p, j, :, 1], halves[:, :], start=(j == 0), stop=False,
                                     skip_group_check=True)
                last = nc.tensor.matmul(p_c[:, 0:BT], ones3[0:1, :], ones3[0:1, 0:BT], start=False, stop=True,
                                        skip_group_check=True)
                last.then_inc(aT_ps, 1)

            def products(turn, off, g):
                i, s, _ = place(turn, off)
                if not first(i, 1):
                    pe.wait_ge(prod_used, 2 * i + g - 1)
                pe.wait_ge(hT_sb, 2 * i + g + 1)
                nc.tensor.matmul(p_s[g][:, :], ones3[:, :], bias3[:, :], start=True, stop=False)
                for j in range(GT):
                    c = slice(P * j, P * j + P)
                    nc.tensor.matmul(p_s[g][:, c], hT[:, s % 2, g, c], wsT[:, :], start=False, stop=(j == GT - 1))
                pe.wait_ge(aT_sb, 2 * i + g + 1)
                for j in range(GT):
                    c = slice(P * j, P * j + P)
                    last = nc.tensor.matmul(p_n[g][:, c], aT[:, s % 2, g, c], wnT[:, :], start=True, stop=True)
                last.then_inc(prod_ready, 1)

            def step0(turn, off):
                i, s, _ = place(turn, off)
                p = s % HR
                if there(turn, off):
                    pe.wait_ge(h_ready[0], 2 * i + 1)
                    transpose_h(i, p, 0)
                    transpose_h(i, p, 1)
                if there(turn, off - 1):
                    products(turn, off - 1, 0)
                if there(turn, off):
                    aggregate(i, p, s)
                if there(turn, off - 1):
                    products(turn, off - 1, 1)

            def step1(turn, off):
                i, s, _ = place(turn, off)
                p = s % HR
                if not there(turn, off):
                    return
                banks = (p_s, p_n)[s % 2]
                pe.wait_ge(h_ready[1], 2 * i + 1)
                if not first(i, 2):
                    pe.wait_ge(y_ready[1], i - 1)
                for g in range(2):
                    nc.tensor.matmul(banks[g][:, :], ident[:, :], H[:, p, g:BT:2, :], start=True, stop=False)
                pe.wait_ge(h_ready[1], 2 * i + 2)
                pe.wait_ge(row_ready[1], i + 1)
                pe.wait_ge(sel_ready[1], i + 1)
                for j in range(GT):
                    for g in range(2):
                        q = slice(SLOTS * g, SLOTS * g + SLOTS)
                        last = nc.tensor.matmul(banks[g][:, P * j:P * j + P], SEL[q, p, j, :], H[q, p, BT + j, :],
                                                start=False, stop=(j == GT - 1))
                last.then_inc(agg_ready, 1)

            def fast():
                schedule(pe, step0)
                schedule(pe, step1)

            def general():
                nc.tensor.matmul(p_n[0][:, 0:2 * D], ones[0:1, :], brow[0:1, :, :].rearrange("p a b -> p (a b)"),
                                 start=True, stop=True).then_inc(g_ord, 1)
                for r in (0, 1, 3):
                    def lot(c):
                        pe.wait_ge(gs["diag"][r], c + 1)
                        nc.tensor.matmul(p_c[0:ER, 0:ER], ones[0:ER, 0:ER], g_diag[0:ER, 0:ER],
                                         start=True, stop=True).then_inc(gs["keys"][r], 1)
                        pe.wait_ge(gs["same"][r], c + 1)
                        pe.wait_ge(gs["msg"][r], c + 1)
                        nc.tensor.matmul(p_s[0][0:ER, 0:XW], g_same[0:ER, 0:ER], g_msg[0:ER, :],
                                         start=True, stop=True).then_inc(gs["sum"][r], 1)

                    if r == 0:
                        pe.wait_ge(g_ord, 2)
                    lot(0)
                    with pe.Fori(1, EC) as c:
                        lot(c)
                    if r != 1:
                        continue

                    def tile(n):
                        pe.wait_ge(gs["msg"][2], n + 1)
                        nc.tensor.transpose(p_T[0][:, 0:P], g_h, ident[:, :])
                        nc.tensor.transpose(p_T[1][:, 0:P], g_own[:, 0:D], ident[:, :]).then_inc(gs["tT"][2], 1)
                        pe.wait_ge(gs["tS"][2], n + 1)
                        nc.tensor.matmul(p_s[0][:, 0:D], g_hT, wsT[:, :], start=True, stop=True)
                        nc.tensor.matmul(p_s[1][:, 0:D], g_aT, wnT[:, :], start=True, stop=True
                                         ).then_inc(gs["prod"][2], 1)

                    tile(0)
                    with pe.Fori(1, NG) as n:
                        tile(n)

            either(pe, fast, general)

        @block.vector
        def _(dve):
            steps = [0, None]
            V = nc.vector

            def wait_steps(step=None):
                step = steps[0] if step is None else step
                dve.wait_ge(s_dve, step if steps[1] is None else steps[1] + step)

            def counted(ins):
                steps[0] += 1
                ins.then_inc(s_dve, 1)
                return steps[0]

            def done(ins):
                wait_steps(counted(ins))

            V.memset(en[:, EC - 1:EC], -1).then_inc(s_end, 1)
            V.memset(eps[:, :], EPS)
            V.memset(ones3[:, :], 1.0)
            V.memset(tail[:, 0, :], float(4 * N))
            V.memset(tail[:, 1, :], 0.0)
            V.memset(ones[:, :], 1.0)
            V.memset(ones_row[:, :], 1.0)
            V.memset(rowsum[:, :], 0.0)
            V.memset(verdict[0:1, 3, :], 0.0)
            done(V.memset(halves[:, :], 0.0))
            V.memset(halves[0:SLOTS, 0:1], 1.0)
            V.memset(halves[SLOTS:P, 1:2], 1.0)
            dve.wait_ge(s_edges, 64)
            V.tensor_copy(edf[:, :], ed[:, :]).then_inc(s_dst, 1)
            dve.wait_ge(s_const, 4)
            done(V.tensor_scalar(start[:, :], tnum[:, :], float(NT - BT), float(-BACK), ALU.is_ge, ALU.mult))
            done(V.scalar_tensor_tensor(start[:, :], tnum[:, :], float(P), start[:, :], ALU.mult, ALU.add))
            V.tensor_scalar(end[:, :], start[:, :], float(P), None, ALU.add)
            dve.wait_ge(s_dst, 1)
            V.tensor_scalar(diag[:, :], ident[0:ER, 0:ER], edf[:, 0:1], None, ALU.mult).then_inc(s_diag, 1)
            done(V.tensor_copy(esf[:, :], es[:, :]))
            dve.wait_ge(s_pe0, 3)
            done(V.tensor_copy(firsts[:, :], p_c[0:TP, 0:ER]))
            done(V.tensor_tensor(below[:, :, :], firsts[:, :].rearrange("p (a c) -> p a c", a=1).to_broadcast([TP, TB, ER]),
                                 start[:, :].rearrange("p (b a) -> p b a", a=1).to_broadcast([TP, TB, ER]), ALU.is_lt))
            done(V.tensor_reduce(rowf[:, :], below[:, :, :], AX.X, ALU.add))
            done(V.tensor_scalar(rowf[:, :], rowf[:, :], -1.0, 0.0, ALU.add, ALU.max))
            V.tensor_copy(rowi[:, :], rowf[:, :]).then_inc(s_rows, 1)
            dve.wait_ge(s_next, 1)
            V.tensor_tensor(em[:, :], edf[:, :], enf[:, :], ALU.not_equal)
            done(V.tensor_tensor(diff[:, 1, :], edf[:, :], esf[:, :], ALU.is_equal))
            done(V.tensor_tensor(em[:, :], em[:, :], diff[:, 1, :], ALU.mult))
            V.scalar_tensor_tensor(esf[:, :], em[:, :], NO_LINK, esf[:, :], ALU.mult, ALU.add).then_inc(s_scr, 1)
            V.tensor_tensor(diff[:, 0, :], edf[:, :], enf[:, :], ALU.is_gt).then_inc(s_marks, 1)
            def cut_digits(first_cut):
                for n in range(first_cut, first_cut + 2):
                    e, k = divmod(n, len(CUTS))
                    if n >= 2:
                        dve.wait_ge(s_digits, n - 1)
                    V.tensor_scalar(part[:, n % 2, :], (es, ed)[e][:, :], CUTS[k], 63, ALU.arith_shift_right,
                                    ALU.bitwise_and).then_inc(s_part, 1)

            for g, group in enumerate(GROUPS):
                dve.wait_ge(s_rowg[g], 16 * len(group))
                for b in group:
                    done(V.tensor_scalar(junk[:, :], drow[:, b, :], start[:, b:b + 1], None, ALU.is_lt, ALU.add,
                                         accum_out=cnt_in[:, b:b + 1]))
                c = slice(group[0], group[-1] + 1)
                done(V.scalar_tensor_tensor(ptr_f[:, c], rowf[:, c], float(EC), cnt_in[:, c], ALU.mult, ALU.add))
                V.tensor_copy(ptr_i[:, c], ptr_f[:, c]).then_inc(s_ptr, 1)
            cut_digits(0)
            for g, group in enumerate(GROUPS):
                if g == 1:
                    cut_digits(4)
                c = slice(group[0], group[-1] + 1)
                w = len(group)
                dve.wait_ge(s_wing[g], 32 * w)
                done(V.tensor_tensor(wd[:, c, :], end[:, c].rearrange("p (b a) -> p b a", a=1).to_broadcast([TP, w, WIN]),
                                     wd[:, c, :], ALU.subtract))
                done(V.scalar_tensor_tensor(wd[:, c, :], wd[:, c, :], float(1 << SHIFT), wl[:, c, :], ALU.mult, ALU.subtract))
                if g == 0:
                    cut_digits(2)
                for r in range(0, SLOTS, 8):
                    for b in group:
                        last = V.max(codes[:, b, r:r + 8], wd[:, b, :])
                    done(last)
                    if r + 8 < SLOTS:
                        for b in group:
                            last = V.match_replace(wd[:, b, :], codes[:, b, r:r + 8], wd[:, b, :], -1.0)
                        done(last)
            V.tensor_scalar(minus[:, :, :], codes[:, :, :], 0.0, -1.0, ALU.max, ALU.mult)
            done(V.scalar_tensor_tensor(filler[:, :, :], codes[:, :, :], 0.0,
                                        start[:, :].rearrange("p (b a) -> p b a", a=1).to_broadcast([TP, TB, SLOTS]),
                                        ALU.is_le, ALU.mult))
            done(V.scalar_tensor_tensor(codei[:, :, :], minus[:, :, :], TOP, filler[:, :, :], ALU.add, ALU.add))
            done(V.tensor_scalar(dli[:, :, :], codei[:, :, :], SHIFT, None, ALU.arith_shift_right))
            V.tensor_scalar(codei[:, :, :], codei[:, :, :], (1 << SHIFT) - 1, None, ALU.bitwise_and).then_inc(s_dl2, 1)
            V.tensor_copy(dl2[:, :, :, :], dli[:, :, :].rearrange("p b (a n) -> p b a n", a=1
                                                                  ).to_broadcast([TP, TB, 2, SLOTS])).then_inc(s_dl2, 1)
            done(V.tensor_scalar(cnt_in[:, :], codes[:, :, SLOTS - 1], 1.0, None, ALU.is_ge))
            done(V.tensor_reduce(rowsum[0:TP, 2:3], cnt_in[:, :], AX.X, ALU.add))
            dve.wait_ge(s_full, 1)
            dve.wait_ge(s_prod_used, len(HASHES))
            for k in range(2):
                last = V.tensor_copy(rowint[:, :, k], rowsum[:, :])
            done(last)
            V.tensor_scalar(rowint[:, :, 0], rowint[:, :, 0], 10, None, ALU.arith_shift_right)
            done(V.tensor_scalar(rowint[:, :, 1], rowint[:, :, 1], 1023, None, ALU.bitwise_and))
            V.tensor_copy(checks[:, :, :], rowint[:, :, :]).then_inc(s_sums, 1)
            dve.wait_ge(s_pe0, 4)
            for o, i in table_parts(DL, p_s):
                last = V.tensor_copy(o, i)
            last.then_inc(s_tab, 1)
            for s in range(HR):
                V.memset(Y[:, s, :, D:XW], 0.0)
            V.memset(verdict[0:1, 2, :], 0.0)
            done(V.memset(verdict[0:1, 0, :], 0.0))
            V.memset(verdict[0:1, 2, 0:1], 1.0)
            V.memset(verdict[0:1, 2, 1:2], float(N))
            dve.wait_ge(s_total, 1)
            total = p_c[0:1, 0:2 * CHECKS].rearrange("p (a b) -> p a b", b=2)
            done(V.tensor_copy(verdict[0:1, 0:2, :], total.rearrange("p a b -> p b a")))
            done(V.scalar_tensor_tensor(verdict[0:1, 0, :], verdict[0:1, 0, :], 1024.0, verdict[0:1, 1, :],
                                        ALU.mult, ALU.add))
            done(V.tensor_tensor(verdict[0:1, 0, :], verdict[0:1, 0, :], verdict[0:1, 2, :], ALU.not_equal))
            done(V.tensor_reduce(bad[0:1, :], verdict[0:1, 0, :], AX.X, ALU.add))
            V.tensor_scalar(flag[0:1, :], bad[0:1, :], 0.0, None, ALU.is_equal).then_inc(s_flag, 1)
            again, upto, links = filler, minus, codes
            V.memset(again[:, :, 0:1], 0.0)
            done(V.tensor_tensor(again[:, :, 1:SLOTS], dli[:, :, 1:SLOTS], dli[:, :, 0:SLOTS - 1], ALU.is_equal))
            done(V.tensor_tensor_scan(upto[:, :, :].rearrange("p b n -> p (b n)"),
                                      again[:, :, :].rearrange("p b n -> p (b n)"),
                                      ones_row[:, :], 0.0, ALU.mult, ALU.add))
            flat = [t[:, :, :].rearrange("p b n -> p (b n)") for t in (links, again, upto)]
            V.tensor_copy(flat[0][:, TB * SLOTS - 1:TB * SLOTS], flat[2][:, TB * SLOTS - 1:TB * SLOTS])
            V.tensor_tensor_scan(flat[0][:, TB * SLOTS - 2::-1], flat[1][:, TB * SLOTS - 1:0:-1],
                                 flat[2][:, TB * SLOTS - 2::-1], flat[2][:, TB * SLOTS - 1:TB * SLOTS],
                                 ALU.mult, ALU.max).then_inc(s_runs, 1)
            dve.wait_ge(s_roots, 1)
            done(V.reciprocal(minus[:, :, :], filler[:, :, :]))
            V.tensor_copy(dis2[:, :, :, :], minus[:, :, :].rearrange("p b (a n) -> p b a n", a=1
                                                                     ).to_broadcast([TP, TB, 2, SLOTS])).then_inc(s_dis2, 1)
            dve.wait_ge(s_tab, 2)

            def stats(l, turn, off):
                i, s, uses = place(turn, off)
                dve.wait_ge(x_loaded[l][s], uses * 16)
                for r in range(0, ROWS, 2):
                    if r == BT:
                        dve.wait_ge(gathered[l][s], uses * (16 * PAIRS))
                    last = V.bn_stats(ST[:, s, r:r + 2, :].rearrange("p r k -> p (r k)"),
                                      X[:, s, r:r + 2, 0:D].rearrange("p r c -> p c r"))
                last.then_inc(st_ready[l], 1)

            def inverse(l, turn, off):
                i, s, _ = place(turn, off)
                dve.wait_ge(sd_ready[l], i + 1)
                return counted(V.reciprocal((scale, rstd)[l][:, s, :], sd[:, s, :]))

            def select(l, turn, off):
                i, s, _ = place(turn, off)
                if not first(i, HR):
                    dve.wait_ge((aT_ps, agg_ready)[l], i - HR + 1)
                V.tensor_tensor(SEL[:, s % HR, :, :],
                                iota_n[:, :].rearrange("p (a n) -> p a n", a=1).to_broadcast([P, PAIRS, P]),
                                DL[:, bass.ds(i * PAIRS, PAIRS)].rearrange("p (a n) -> p a n", n=1).to_broadcast([P, PAIRS, P]),
                                ALU.is_equal).then_inc(sel_ready[l], 1)

            def factors(turn, off):
                i, s, _ = place(turn, off)
                V.tensor_tensor(factor[:, s, 0:BT], X[:, s, 0:BT, D], X[:, s, 0:BT, D], ALU.mult)
                return counted(V.tensor_tensor(factor[:, s, BT:ROWS], X[:, s, BT:ROWS, D],
                                               DISL[:, bass.ds(i * PAIRS, PAIRS)], ALU.mult))

            def scales1(turn, off, inverted):
                i, s, _ = place(turn, off)
                wait_steps(inverted)
                return counted(V.tensor_tensor(scale[:, s, :], rstd[:, s, :], factor[:, s, :], ALU.mult))

            def shifts(l, turn, off, before):
                i, s, _ = place(turn, off)
                wait_steps(before)
                V.scalar_tensor_tensor(shift[:, s, :], ST[:, s, :, 1], -1.0, scale[:, s, :], ALU.mult, ALU.mult
                                       ).then_inc(norm_ready[l], 1)

            def scaled(turn, off, g):
                i, s, _ = place(turn, off)
                y = s % HR
                if g == 0 and not first(i, HR):
                    dve.wait_ge(stored[0][y], stores_before(turn, off) * 16)
                dve.wait_ge(prod_ready, 2 * i + g + 1)
                for j in range(GT):
                    t = 2 * j + g
                    last = V.scalar_tensor_tensor(Y[:, y, t, 0:D], p_n[g][:, P * j:P * j + P], rc[:, s % 2, t:t + 1],
                                                  X[:, s, t, 0:D], ALU.mult, ALU.add)
                return counted(last)

            def added(turn, off, g, scaled_by):
                i, s, _ = place(turn, off)
                wait_steps(scaled_by)
                o = Y[:, s % HR, g:BT:2, 0:D]
                V.tensor_tensor(o, o, p_s[g][:, :].rearrange("p (a b) -> p a b", a=GT), ALU.add
                                ).then_inc(prod_used, 1)

            def dis(turn, off):
                i, s, _ = place(turn, off)
                dve.wait_ge(sdeg_ready, i + 1)
                V.reciprocal(Y[:, s % HR, :, D], sdeg[:, s % 2, :]).then_inc(y_ready[0], 1)

            def stores_before(turn, off):
                return turn * (RING // HR) + off // HR

            def inverse_counts(turn, off):
                i, s, _ = place(turn, off)
                dve.wait_ge(aT_ps, i + 1)
                V.reciprocal(rc[:, s % 2, :], p_c[:, 0:BT]).then_inc(counts_read, 1)

            def scale_row(turn, off):
                i, s, _ = place(turn, off)
                r = ROWS - 1
                dve.wait_ge(norm_ready[1], i + 1)
                if not first(i, HR):
                    dve.wait_ge(agg_ready, i - HR + 1)
                V.tensor_scalar(H[:, s % HR, r, :], X[:, s, r, 0:D], scale[:, s, r:r + 1], shift[:, s, r:r + 1],
                                ALU.mult, ALU.add).then_inc(row_scaled[1], 1)

            def relu_row(turn, off):
                i, s, _ = place(turn, off)
                r = ROWS - 1
                dve.wait_ge(row_scaled[1], i + 1)
                V.tensor_scalar(H[:, s % HR, r, :], H[:, s % HR, r, :], 0.0, None, ALU.max).then_inc(row_ready[1], 1)

            def finish1(turn, off, g):
                i, s, _ = place(turn, off)
                y = s % HR
                if g == 0:
                    if first(i, HR):
                        dve.wait_ge(stored[0][y], 16 * len(range(y, NB, HR)))
                    else:
                        dve.wait_ge(stored[1][y], stores_before(turn, off) * 16)
                    dve.wait_ge(agg_ready, i + 1)
                bank = (p_s, p_n)[s % 2][g]
                last = V.scalar_tensor_tensor(Y[:, y, g:BT:2, 0:D], bank[:, :].rearrange("p (a b) -> p a b", a=GT), 0.0,
                                              X[:, s, g:BT:2, 0:D], ALU.max, ALU.add)
                if g == 1:
                    last.then_inc(y_ready[1], 1)

            def step0(turn, off):
                before, this = there(turn, off - 2), there(turn, off - 1)
                if before:
                    odd = scaled(turn, off - 2, 1)
                if this:
                    inverse_counts(turn, off - 1)
                if before:
                    added(turn, off - 2, 1, odd)
                if before:
                    dis(turn, off - 2)
                if there(turn, off + STATS_AHEAD):
                    stats(0, turn, off + STATS_AHEAD)
                if there(turn, off + 2):
                    inverted = inverse(0, turn, off + 2)
                if this:
                    dve.wait_ge(counts_read, place(turn, off - 1)[0] + 1)
                    even = scaled(turn, off - 1, 0)
                if there(turn, off + 1):
                    select(0, turn, off + 1)
                if there(turn, off + 2):
                    shifts(0, turn, off + 2, inverted)
                if this:
                    added(turn, off - 1, 0, even)

            def step1(turn, off):
                if there(turn, off + 1):
                    scale_row(turn, off + 1)
                if there(turn, off + STATS_AHEAD):
                    stats(1, turn, off + STATS_AHEAD)
                if there(turn, off + 1):
                    relu_row(turn, off + 1)
                if there(turn, off + 2):
                    factors(turn, off + 2)
                    inverted = inverse(1, turn, off + 2)
                if there(turn, off + 1):
                    select(1, turn, off + 1)
                if there(turn, off + 2):
                    scale_of = scales1(turn, off + 2, inverted)
                if there(turn, off - 1):
                    finish1(turn, off - 1, 0)
                if there(turn, off + 2):
                    shifts(1, turn, off + 2, scale_of)
                if there(turn, off - 1):
                    finish1(turn, off - 1, 1)

            def fast():
                PER_STEP = (3, 3)
                for l, step in enumerate((step0, step1)):
                    for off in range(-AHEAD, RING):
                        step(0, off)
                    at = steps[0]
                    with dve.Fori(1, ITERS) as turn:
                        steps[1] = (turn - 1) * (RING * PER_STEP[l])
                        for off in range(RING):
                            step(turn, off)
                    steps[1] = None
                    assert steps[0] == at + RING * PER_STEP[l]
                    steps[0] += (ITERS - 2) * RING * PER_STEP[l]
                    for off in range(ITERS * RING, NB + 2):
                        step(0, off)

            def general():
                order = [0, None]

                def then(ins):
                    order[0] += 1
                    ins.then_inc(g_ord, 1)
                    dve.wait_ge(g_ord, order[0] if order[1] is None else order[1] + order[0])

                for s in range(RING):
                    dve.wait_ge(x_loaded[0][s], 16)
                dve.wait_ge(g_ord, 1)
                order[0] = 1
                V.memset(work[:, :], 0.0).then_inc(g_clean, 1)
                dve.wait_ge(g_clean, 1)
                V.tensor_copy(g_bs, p_n[0][:, 0:D])
                then(V.tensor_copy(g_bn, p_n[0][:, D:2 * D]))

                def norm(r, c, rows, by):
                    V_ = slice(0, rows)
                    then(V.bn_stats(g_st[V_, :], g_rows[V_, 0:D]))
                    dve.sem_inc(g_clean, 1)
                    V.bn_aggr(g_mv[V_, :], g_st[V_, :]).then_inc(gs["var"][r], 1)
                    dve.wait_ge(gs["sd"][r], c + 1)
                    then(V.reciprocal(g_rs[V_, :], g_sd[V_, :]))
                    then(V.tensor_scalar(g_t1[V_, :], g_rows[V_, 0:D], g_mv[V_, 0:1], g_rs[V_, :], ALU.subtract, ALU.mult))
                    then(V.tensor_scalar(g_h[V_, :], g_t1[V_, :], 0.0, by, ALU.max, ALU.mult))

                def lot(r, c):
                    key, other = ((es, ed), (ed, es), None, (ed, es))[r]
                    V.tensor_copy(g_idx[0:ER, 0:1], key[:, bass.ds(c, 1)])
                    then(V.tensor_copy(g_idx[0:ER, 1:2], other[:, bass.ds(c, 1)]))
                    V.tensor_copy(g_keyf[0:ER, :], g_idx[0:ER, 0:1]).then_inc(gs["idx"][r], 1)
                    dve.wait_ge(gs["idx"][r], c + 1)
                    V.tensor_scalar(g_diag[0:ER, 0:ER], ident[0:ER, 0:ER], g_keyf[0:ER, :], None, ALU.mult
                                    ).then_inc(gs["diag"][r], 1)
                    dve.wait_ge(gs["keys"][r], c + 1)
                    V.tensor_scalar(g_same[0:ER, 0:ER], p_c[0:ER, 0:ER], g_keyf[0:ER, :], None, ALU.is_equal
                                    ).then_inc(gs["same"][r], 1)
                    if r != 1:
                        dve.wait_ge(gs["got"][r], 16 * c + 16)
                        norm(r, c, ER, 1.0 if r == 0 else g_rows[0:ER, D:D + 1])
                        then(V.tensor_copy(g_msg[0:ER, 0:D], g_h[0:ER, :]))
                    V.memset(g_msg[0:ER, D:D + 1], 0.0 if r == 3 else 1.0).then_inc(gs["msg"][r], 1)
                    dve.wait_ge(gs["old"][r], 16 * c + 16)
                    dve.wait_ge(gs["sum"][r], c + 1)
                    V.tensor_tensor(g_new[0:ER, :], p_s[0][0:ER, 0:XW], g_acc[0:ER, :], ALU.add
                                    ).then_inc(gs["new"][r], 1)
                    dve.wait_ge(gs["put"][r], 16 * c + 16)

                def tile(r, n):
                    dve.wait_ge(gs["got"][r], 48 * n + 48)
                    if r == 4:
                        then(V.tensor_scalar(g_t1, g_own[:, 0:D], g_rows[:, D:D + 1], 0.0, ALU.mult, ALU.max))
                        V.tensor_tensor(g_y[:, 0:D], g_rows[:, 0:D], g_t1, ALU.add).then_inc(gs["new"][r], 1)
                        return
                    then(V.tensor_scalar(g_c[:, 0:1], g_own[:, D:D + 1], 1.0, None, ALU.max))
                    V.reciprocal(g_c[:, 3:4], g_c[:, 0:1])
                    V.tensor_scalar(g_c[:, 1:2], g_in[:, D:D + 1], 1.0, None, ALU.max).then_inc(gs["diag"][r], 1)
                    norm(r, n, P, 1.0)
                    dve.sem_inc(gs["msg"][r], 1)
                    dve.wait_ge(gs["tT"][r], n + 1)
                    V.tensor_copy(g_hT, p_T[0][:, 0:P])
                    V.tensor_copy(g_aT, p_T[1][:, 0:P]).then_inc(gs["tS"][r], 1)
                    dve.wait_ge(gs["prod"][r], n + 1)
                    then(V.tensor_scalar(g_t1, g_bn, g_own[:, D:D + 1], None, ALU.mult))
                    then(V.tensor_tensor(g_t1, p_s[1][:, 0:D], g_t1, ALU.add))
                    then(V.scalar_tensor_tensor(g_t1, g_t1, g_c[:, 3:4], g_rows[:, 0:D], ALU.mult, ALU.add))
                    then(V.tensor_tensor(g_t2, p_s[0][:, 0:D], g_bs, ALU.add))
                    V.tensor_tensor(g_y[:, 0:D], g_t1, g_t2, ALU.add)
                    dve.wait_ge(gs["keys"][r], n + 1)
                    then(V.reciprocal(g_c[:, 0:1], g_c[:, 2:3]))
                    V.scalar_tensor_tensor(g_y[:, D:D + 1], g_in[:, D:D + 1], 0.0, g_c[:, 0:1], ALU.is_gt, ALU.mult
                                           ).then_inc(gs["new"][r], 1)

                for r in range(5):
                    step_of, n = (tile, NG) if r in (2, 4) else (lot, EC)
                    if r in (1,):
                        then(V.memset(g_msg, 0.0))
                    before = order[0]
                    step_of(r, 0)
                    per = order[0] - before
                    with dve.Fori(1, n) as c:
                        order[1] = (c - 1) * per
                        step_of(r, c)
                    order[1] = None
                    order[0] += (n - 2) * per

            either(dve, fast, general)


_INS = ['x', 'src', 'dst', 'L0_gnn_W_self', 'L0_gnn_b_self', 'L0_gnn_W_neigh', 'L0_gnn_b_neigh']


def kernel(**inputs):
    import numpy as _np
    import concourse.bacc as _bacc
    from concourse.bass_utils import run_bass_kernel_spmd as _run

    nc = _bacc.Bacc("TRN2", target_bir_lowering=False, num_devices=1)
    arrays, args = {}, []
    for name in _INS:
        a = _np.ascontiguousarray(inputs[name])
        arrays[f"in_{name}"] = a
        args.append(nc.dram_tensor(f"in_{name}", a.shape, mybir.dt.from_np(a.dtype), kind="ExternalInput").ap())
    out = nc.dram_tensor("out_x", arrays["in_x"].shape, f32, kind="ExternalOutput").ap()
    gnn(nc, *args, out)
    r = _run(nc, [arrays], core_ids=[0])
    return r.results[0]["out_x"]
```
